# Optimizing a Trainium2 kernel written in Bass

```python
import numpy as np
import jax
import jax.numpy as jnp

def _softmax(x, axis=-1):
    return jax.nn.softmax(x, axis=axis)

def _gelu(x):
    return jax.nn.gelu(x, approximate=True)

def _silu(x):
    return jax.nn.silu(x)

def _sigmoid(x):
    return jax.nn.sigmoid(x)

def _layernorm(x, axis=-1, eps=1e-05):
    m = jnp.mean(x, axis=axis, keepdims=True)
    v = jnp.var(x, axis=axis, keepdims=True)
    return (x - m) / jnp.sqrt(v + eps)

def _scatter_add(tgt, idx, src, axis=0):
    return tgt.at[idx].add(src)

def _segment_sum(src, seg, n):
    return jax.ops.segment_sum(src, seg, n)
kernel_name = 'mk_xattn_ffn_d4_seqx_r4_b2518b'

def setup_inputs(seed: int=0):
    np.random.seed(seed)
    _w = jnp.asarray

    def _rec_inputs():
        import jax
        import jax.numpy as jnp
        _rk = jax.random.key(seed)
        x = -0.0002928 + 1 * jax.random.normal(jax.random.fold_in(_rk, 1), (8, 256, 256), jnp.float32)
        _lenS = 256 - jax.random.randint(jax.random.fold_in(_rk, 7), (8,), 0, max(1, 256 // 4) + 1, jnp.int32)
        _lenS2 = 256 - jax.random.randint(jax.random.fold_in(_rk, 8), (8,), 0, max(1, 256 // 4) + 1, jnp.int32)
        _ctx_1024P = jax.random.normal(jax.random.fold_in(_rk, 11), (8, 16, 256), jnp.float32)
        _ctx_1024c = jax.random.dirichlet(jax.random.fold_in(_rk, 511), 0.3 * jnp.ones((16,), jnp.float32), (8, 256))
        _ctx_1024t = jnp.einsum('bsk,bkd->bsd', _ctx_1024c, _ctx_1024P)
        _ctx_1024t = _ctx_1024t * jax.lax.rsqrt(jnp.mean(jnp.square(_ctx_1024t)) + 1e-12) * 0.953939
        ctx_1024 = -1.39393e-06 + 0.999914 * (_ctx_1024t + 0.3 * jax.random.normal(jax.random.fold_in(_rk, 611), (8, 256, 256), jnp.float32))
        _validS = jnp.arange(256)[None, :] < _lenS[:, None]
        _validS2 = jnp.arange(256)[None, :] < _lenS2[:, None]
        _causal = jnp.tril(jnp.ones((256, 256), dtype=bool))
        mask_BxSxS2_ik0 = jnp.where(jnp.broadcast_to(_validS2[:, None, :], (8, 256, 256)), 0, 1).astype(jnp.int32)
        return (x, ctx_1024, mask_BxSxS2_ik0)
    x, ctx_1024, mask_BxSxS2_ik0 = _rec_inputs()

    def _L0_xattn_setup():
        import jax, jax.numpy as jnp
        import numpy as np
        EMBED_PHI = 256
        EMBED_F = 256
        HIDDEN_F = 256
        N_HEADS = 16
        B, S = (2, 512)
        key = jax.random.key(seed)
        ks = jax.random.split(key, 9)
        sphi = 1.0 / np.sqrt(EMBED_PHI)
        sf = 1.0 / np.sqrt(EMBED_F)
        sh = 1.0 / np.sqrt(HIDDEN_F)
        return {'q': jax.random.normal(ks[0], (B, S, EMBED_PHI), jnp.float32), 'k': jax.random.normal(ks[1], (B, S, EMBED_PHI), jnp.float32), 'v': jax.random.normal(ks[2], (B, S, EMBED_F), jnp.float32), 'Wq': jax.random.normal(ks[3], (HIDDEN_F, EMBED_PHI), jnp.float32) * sphi, 'Wk': jax.random.normal(ks[4], (HIDDEN_F, EMBED_PHI), jnp.float32) * sphi, 'Wv': jax.random.normal(ks[5], (HIDDEN_F, EMBED_F), jnp.float32) * sf, 'bv': jax.random.normal(ks[6], (HIDDEN_F,), jnp.float32) * sf, 'Wo': jax.random.normal(ks[7], (EMBED_F, HIDDEN_F), jnp.float32) * sh, 'bo': jax.random.normal(ks[8], (EMBED_F,), jnp.float32) * sh}
    _L0_xattn_all = _L0_xattn_setup()
    _L0_xattn_in = {k: v for k, v in _L0_xattn_all.items() if k in ('Wq', 'Wk', 'Wv', 'bv', 'Wo', 'bo')}
    del _L0_xattn_all

    def _L0_ffn_setup():
        import jax, jax.numpy as jnp
        import numpy as np
        key = jax.random.key(seed)
        kx, kw = jax.random.split(key)
        x = jax.random.normal(kx, (32, 1024, 256), dtype=jnp.float32)
        weight = jax.random.normal(kw, (256, 256), dtype=jnp.float32) * 0.01
        return {'x': x, 'weight': weight}
    _L0_ffn_all = _L0_ffn_setup()
    _L0_ffn_in = {k: v for k, v in _L0_ffn_all.items() if k in ('weight',)}
    del _L0_ffn_all

    def _L1_xattn_setup():
        import jax, jax.numpy as jnp
        import numpy as np
        import math
        D_MODEL = 256
        N_HEADS = 16
        key = jax.random.key(seed)
        ks = jax.random.split(key, 11)
        N, L, S = (2, 512, 512)
        d = D_MODEL
        s = 1.0 / math.sqrt(d)
        return {'queries': jax.random.normal(ks[0], (N, L, d), dtype=jnp.float32), 'keys': jax.random.normal(ks[1], (N, S, d), dtype=jnp.float32), 'values': jax.random.normal(ks[2], (N, S, d), dtype=jnp.float32), 'Wq': jax.random.normal(ks[3], (d, d), dtype=jnp.float32) * s, 'bq': jax.random.normal(ks[4], (d,), dtype=jnp.float32) * s, 'Wk': jax.random.normal(ks[5], (d, d), dtype=jnp.float32) * s, 'bk': jax.random.normal(ks[6], (d,), dtype=jnp.float32) * s, 'Wv': jax.random.normal(ks[7], (d, d), dtype=jnp.float32) * s, 'bv': jax.random.normal(ks[8], (d,), dtype=jnp.float32) * s, 'Wo': jax.random.normal(ks[9], (d, d), dtype=jnp.float32) * s, 'bo': jax.random.normal(ks[10], (d,), dtype=jnp.float32) * s}
    _L1_xattn_all = _L1_xattn_setup()
    _L1_xattn_in = {k: v for k, v in _L1_xattn_all.items() if k in ('Wq', 'bq', 'Wk', 'bk', 'Wv', 'bv', 'Wo', 'bo')}
    del _L1_xattn_all

    def _L1_ffn_setup():
        import jax, jax.numpy as jnp
        import numpy as np
        B, S, H = (2, 256, 256)
        E, I = (16, 128)
        TOP_K = 2
        N_SHARED = 2
        SCALE = 1.0
        IS = I * N_SHARED
        key = jax.random.key(seed)
        ks = jax.random.split(key, 8)
        sd = 0.02
        return {'hidden_states': jax.random.normal(ks[0], (B, S, H), jnp.float32), 'gate_w': jax.random.normal(ks[1], (E, H), jnp.float32) * sd, 'w_gate': jax.random.normal(ks[2], (E, H, I), jnp.float32) * sd, 'w_up': jax.random.normal(ks[3], (E, H, I), jnp.float32) * sd, 'w_down': jax.random.normal(ks[4], (E, I, H), jnp.float32) * sd, 'ws_gate': jax.random.normal(ks[5], (H, IS), jnp.float32) * sd, 'ws_up': jax.random.normal(ks[6], (H, IS), jnp.float32) * sd, 'ws_down': jax.random.normal(ks[7], (IS, H), jnp.float32) * sd}
    _L1_ffn_all = _L1_ffn_setup()
    _L1_ffn_in = {k: v for k, v in _L1_ffn_all.items() if k in ('gate_w', 'w_gate', 'w_up', 'w_down', 'ws_gate', 'ws_up', 'ws_down')}
    del _L1_ffn_all

    def _L2_xattn_setup():
        import jax, jax.numpy as jnp
        import numpy as np
        D_MODEL = 256
        HEADS = 16
        D_K = D_MODEL // HEADS
        LN_EPS = 1e-06
        NEG_INF = -1000000000.0

        def _layernorm(x, scale, bias):
            mu = jnp.mean(x, axis=-1, keepdims=True)
            var = jnp.var(x, axis=-1, keepdims=True)
            return (x - mu) * jax.lax.rsqrt(var + LN_EPS) * scale + bias
        key = jax.random.key(seed)
        ks = jax.random.split(key, 8)
        bs, sq, skv = (4, 512, 512)
        init = 1.0 / np.sqrt(D_MODEL)
        return {'kv': jax.random.normal(ks[0], (bs, skv, D_MODEL), jnp.float32), 'q': jax.random.normal(ks[1], (bs, sq, D_MODEL), jnp.float32), 'mask': jax.random.randint(ks[2], (bs, sq, skv), 0, 2, jnp.int32), 'Wq': jax.random.normal(ks[3], (D_MODEL, D_MODEL), jnp.float32) * init, 'bq': jnp.zeros((D_MODEL,), jnp.float32), 'Wk': jax.random.normal(ks[4], (D_MODEL, D_MODEL), jnp.float32) * init, 'bk': jnp.zeros((D_MODEL,), jnp.float32), 'Wv': jax.random.normal(ks[5], (D_MODEL, D_MODEL), jnp.float32) * init, 'bv': jnp.zeros((D_MODEL,), jnp.float32), 'qn_scale': jnp.ones((D_MODEL,), jnp.float32), 'qn_bias': jnp.zeros((D_MODEL,), jnp.float32), 'kn_scale': jnp.ones((D_MODEL,), jnp.float32), 'kn_bias': jnp.zeros((D_MODEL,), jnp.float32), 'vn_scale': jnp.ones((D_MODEL,), jnp.float32), 'vn_bias': jnp.zeros((D_MODEL,), jnp.float32), 'Wo': jax.random.normal(ks[6], (D_MODEL, D_MODEL), jnp.float32) * init, 'bo': jnp.zeros((D_MODEL,), jnp.float32)}
    _L2_xattn_all = _L2_xattn_setup()
    _L2_xattn_in = {k: v for k, v in _L2_xattn_all.items() if k in ('Wq', 'bq', 'Wk', 'bk', 'Wv', 'bv', 'qn_scale', 'qn_bias', 'kn_scale', 'kn_bias', 'vn_scale', 'vn_bias', 'Wo', 'bo')}
    del _L2_xattn_all

    def _L2_ffn_setup():
        import jax, jax.numpy as jnp
        import numpy as np
        HIDDEN = 256
        INNER = 1024

        def _weight_quant(w):
            scale = 1.0 / jnp.clip(jnp.mean(jnp.abs(w)), 1e-05)
            wq = jnp.clip(jnp.round(w * scale), -1.0, 1.0) / scale
            return w + jax.lax.stop_gradient(wq - w)

        def _act_quant(x):
            scale = 127.0 / jnp.clip(jnp.max(jnp.abs(x), axis=-1, keepdims=True), 1e-05)
            xq = jnp.clip(jnp.round(x * scale), -128.0, 127.0) / scale
            return x + jax.lax.stop_gradient(xq - x)

        def _bitlinear(x, w):
            return jnp.einsum('bsi,oi->bso', _act_quant(x), _weight_quant(w))
        key = jax.random.key(seed)
        k0, k1, k2, k3 = jax.random.split(key, 4)
        x = jax.random.normal(k0, (4, 512, HIDDEN), dtype=jnp.float32)
        w_gate = jax.random.normal(k1, (INNER, HIDDEN), dtype=jnp.float32) / np.sqrt(HIDDEN)
        w_up = jax.random.normal(k2, (INNER, HIDDEN), dtype=jnp.float32) / np.sqrt(HIDDEN)
        w_down = jax.random.normal(k3, (HIDDEN, INNER), dtype=jnp.float32) / np.sqrt(INNER)
        return {'x': x, 'w_gate': w_gate, 'w_up': w_up, 'w_down': w_down}
    _L2_ffn_all = _L2_ffn_setup()
    _L2_ffn_in = {k: v for k, v in _L2_ffn_all.items() if k in ('w_gate', 'w_up', 'w_down')}
    del _L2_ffn_all

    def _L3_xattn_setup():
        import jax, jax.numpy as jnp
        import numpy as np
        NUM_HEADS = 16
        key = jax.random.key(seed)
        kq, kk, kv = jax.random.split(key, 3)
        B, S, DIM = (2, 512, 256)
        q = jax.random.normal(kq, (B, S, DIM), dtype=jnp.float32)
        k = jax.random.normal(kk, (B, S, DIM), dtype=jnp.float32)
        v = jax.random.normal(kv, (B, S, DIM), dtype=jnp.float32)
        return {'q': q, 'k': k, 'v': v}
    _L3_xattn_all = _L3_xattn_setup()
    _L3_xattn_in = {k: v for k, v in _L3_xattn_all.items() if k in ()}
    del _L3_xattn_all

    def _L3_ffn_setup():
        import jax, jax.numpy as jnp
        import numpy as np
        GROUP = 16
        EPS = 1e-05

        def _dequant(q, scale):
            w = q.astype(jnp.float32) / 7.5 - 1.0
            return w * jnp.repeat(scale, GROUP, axis=1)

        def _qlora_linear(x, q, scale, bias, la, lb):
            w = _dequant(q, scale)
            base = jnp.einsum('btd,od->bto', x, w) + bias
            lora = jnp.einsum('btr,or->bto', jnp.einsum('btd,rd->btr', x, la), lb)
            return base + lora

        def _layernorm(x, g, b):
            mu = jnp.mean(x, axis=-1, keepdims=True)
            var = jnp.mean(jnp.square(x - mu), axis=-1, keepdims=True)
            return (x - mu) * jax.lax.rsqrt(var + EPS) * g + b
        key = jax.random.key(seed)
        ks = jax.random.split(key, 6)
        D, R, B, T = (256, 32, 8, 1024)
        x = jax.random.normal(ks[0], (B, T, D), dtype=jnp.float32)
        qweights = jax.random.randint(ks[1], (6, D, D), 0, 16, dtype=jnp.int32)
        scales = jax.random.uniform(ks[2], (6, D, D // GROUP), dtype=jnp.float32)
        biases = jax.random.normal(ks[3], (6, D), dtype=jnp.float32) * 0.02
        lora_a = jax.random.normal(ks[4], (6, R, D), dtype=jnp.float32) * 0.02
        lora_b = jax.random.normal(ks[5], (6, D, R), dtype=jnp.float32) * 0.02
        ln_gamma = jnp.ones((3, D), dtype=jnp.float32)
        ln_beta = jnp.zeros((3, D), dtype=jnp.float32)
        return {'x': x, 'qweights': qweights, 'scales': scales, 'biases': biases, 'lora_a': lora_a, 'lora_b': lora_b, 'ln_gamma': ln_gamma, 'ln_beta': ln_beta}
    _L3_ffn_all = _L3_ffn_setup()
    _L3_ffn_in = {k: v for k, v in _L3_ffn_all.items() if k in ('qweights', 'scales', 'biases', 'lora_a', 'lora_b', 'ln_gamma', 'ln_beta')}
    del _L3_ffn_all
    return {'x': x, 'ctx_1024': ctx_1024, 'mask_BxSxS2_ik0': mask_BxSxS2_ik0, 'L0_xattn_Wq': _L0_xattn_in['Wq'], 'L0_xattn_Wk': _L0_xattn_in['Wk'], 'L0_xattn_Wv': _L0_xattn_in['Wv'], 'L0_xattn_bv': _L0_xattn_in['bv'], 'L0_xattn_Wo': _L0_xattn_in['Wo'], 'L0_xattn_bo': _L0_xattn_in['bo'], 'L0_ffn_weight': _L0_ffn_in['weight'], 'L1_xattn_Wq': _L1_xattn_in['Wq'], 'L1_xattn_bq': _L1_xattn_in['bq'], 'L1_xattn_Wk': _L1_xattn_in['Wk'], 'L1_xattn_bk': _L1_xattn_in['bk'], 'L1_xattn_Wv': _L1_xattn_in['Wv'], 'L1_xattn_bv': _L1_xattn_in['bv'], 'L1_xattn_Wo': _L1_xattn_in['Wo'], 'L1_xattn_bo': _L1_xattn_in['bo'], 'L1_ffn_gate_w': _L1_ffn_in['gate_w'], 'L1_ffn_w_gate': _L1_ffn_in['w_gate'], 'L1_ffn_w_up': _L1_ffn_in['w_up'], 'L1_ffn_w_down': _L1_ffn_in['w_down'], 'L1_ffn_ws_gate': _L1_ffn_in['ws_gate'], 'L1_ffn_ws_up': _L1_ffn_in['ws_up'], 'L1_ffn_ws_down': _L1_ffn_in['ws_down'], 'L2_xattn_Wq': _L2_xattn_in['Wq'], 'L2_xattn_bq': _L2_xattn_in['bq'], 'L2_xattn_Wk': _L2_xattn_in['Wk'], 'L2_xattn_bk': _L2_xattn_in['bk'], 'L2_xattn_Wv': _L2_xattn_in['Wv'], 'L2_xattn_bv': _L2_xattn_in['bv'], 'L2_xattn_qn_scale': _L2_xattn_in['qn_scale'], 'L2_xattn_qn_bias': _L2_xattn_in['qn_bias'], 'L2_xattn_kn_scale': _L2_xattn_in['kn_scale'], 'L2_xattn_kn_bias': _L2_xattn_in['kn_bias'], 'L2_xattn_vn_scale': _L2_xattn_in['vn_scale'], 'L2_xattn_vn_bias': _L2_xattn_in['vn_bias'], 'L2_xattn_Wo': _L2_xattn_in['Wo'], 'L2_xattn_bo': _L2_xattn_in['bo'], 'L2_ffn_w_gate': _L2_ffn_in['w_gate'], 'L2_ffn_w_up': _L2_ffn_in['w_up'], 'L2_ffn_w_down': _L2_ffn_in['w_down'], 'L3_ffn_qweights': _L3_ffn_in['qweights'], 'L3_ffn_scales': _L3_ffn_in['scales'], 'L3_ffn_biases': _L3_ffn_in['biases'], 'L3_ffn_lora_a': _L3_ffn_in['lora_a'], 'L3_ffn_lora_b': _L3_ffn_in['lora_b'], 'L3_ffn_ln_gamma': _L3_ffn_in['ln_gamma'], 'L3_ffn_ln_beta': _L3_ffn_in['ln_beta']}

def reference(x, ctx_1024, mask_BxSxS2_ik0, L0_xattn_Wq, L0_xattn_Wk, L0_xattn_Wv, L0_xattn_bv, L0_xattn_Wo, L0_xattn_bo, L0_ffn_weight, L1_xattn_Wq, L1_xattn_bq, L1_xattn_Wk, L1_xattn_bk, L1_xattn_Wv, L1_xattn_bv, L1_xattn_Wo, L1_xattn_bo, L1_ffn_gate_w, L1_ffn_w_gate, L1_ffn_w_up, L1_ffn_w_down, L1_ffn_ws_gate, L1_ffn_ws_up, L1_ffn_ws_down, L2_xattn_Wq, L2_xattn_bq, L2_xattn_Wk, L2_xattn_bk, L2_xattn_Wv, L2_xattn_bv, L2_xattn_qn_scale, L2_xattn_qn_bias, L2_xattn_kn_scale, L2_xattn_kn_bias, L2_xattn_vn_scale, L2_xattn_vn_bias, L2_xattn_Wo, L2_xattn_bo, L2_ffn_w_gate, L2_ffn_w_up, L2_ffn_w_down, L3_ffn_qweights, L3_ffn_scales, L3_ffn_biases, L3_ffn_lora_a, L3_ffn_lora_b, L3_ffn_ln_gamma, L3_ffn_ln_beta):
    import jax
    import jax.numpy as jnp

    def _L0_xattn_ref(q, k, v, Wq, Wk, Wv, bv, Wo, bo):
        import jax, jax.numpy as jnp
        import numpy as np
        EMBED_PHI = 256
        EMBED_F = 256
        HIDDEN_F = 256
        N_HEADS = 16
        B, S = (2, 512)
        Bq, Sq, _ = q.shape
        hd = HIDDEN_F // N_HEADS
        scale = 1.0 / np.sqrt(hd)
        qh = (q @ Wq.T).reshape(Bq, Sq, N_HEADS, hd).transpose(0, 2, 1, 3)
        kh = (k @ Wk.T).reshape(Bq, Sq, N_HEADS, hd).transpose(0, 2, 1, 3)
        vh = (v @ Wv.T + bv).reshape(Bq, Sq, N_HEADS, hd).transpose(0, 2, 1, 3)
        scores = jnp.einsum('bhsd,bhtd->bhst', qh, kh) * scale
        mask = jnp.triu(jnp.ones((Sq, Sq), dtype=bool), k=0).at[0, 0].set(False)
        scores = jnp.where(mask, -jnp.inf, scores)
        probs = jax.nn.softmax(scores, axis=-1)
        out = jnp.einsum('bhst,bhtd->bhsd', probs, vh)
        out = out.transpose(0, 2, 1, 3).reshape(Bq, Sq, HIDDEN_F)
        return out @ Wo.T + bo

    def _L0_ffn_ref(x, weight):
        import jax, jax.numpy as jnp
        import numpy as np
        b_weight = jnp.sign(weight)
        return jnp.einsum('bsi,oi->bso', x, b_weight)

    def _L1_xattn_ref(queries, keys, values, Wq, bq, Wk, bk, Wv, bv, Wo, bo):
        import jax, jax.numpy as jnp
        import numpy as np
        import math
        D_MODEL = 256
        N_HEADS = 16
        N, L, _ = queries.shape
        S = keys.shape[1]
        H = N_HEADS
        q = (queries @ Wq.T + bq).reshape(N, L, H, -1)
        k = (keys @ Wk.T + bk).reshape(N, S, H, -1)
        v = (values @ Wv.T + bv).reshape(N, S, H, -1)
        D = k.shape[-1]
        sm = jnp.einsum('nlhd,nshd->nlhs', q, k) / math.sqrt(D)
        causal_mask = jnp.triu(jnp.ones((L, S), dtype=bool), k=1)
        sm = jnp.where(causal_mask[None, :, None, :], -jnp.inf, sm)
        sm = jax.nn.softmax(sm, axis=-1)
        attn = jnp.einsum('nlhs,nshd->nlhd', sm, v)
        new_values = attn.reshape(N, L, H * D)
        return new_values @ Wo.T + bo

    def _L1_ffn_ref(hidden_states, gate_w, w_gate, w_up, w_down, ws_gate, ws_up, ws_down):
        import jax, jax.numpy as jnp
        import numpy as np
        B, S, H = (2, 256, 256)
        E, I = (16, 128)
        TOP_K = 2
        N_SHARED = 2
        SCALE = 1.0
        IS = I * N_SHARED
        b, s, h = hidden_states.shape
        x = hidden_states.reshape(-1, h)
        T = x.shape[0]
        logits = jnp.einsum('th,eh->te', x.astype(jnp.float32), gate_w.astype(jnp.float32))
        scores = jax.nn.softmax(logits, axis=-1)
        topk_w, topk_idx = jax.lax.top_k(scores, TOP_K)
        topk_w = topk_w * SCALE
        combine = jnp.zeros((T, E), jnp.float32).at[jnp.arange(T)[:, None], topk_idx].add(topk_w)
        g = jnp.einsum('th,ehi->tei', x, w_gate)
        u = jnp.einsum('th,ehi->tei', x, w_up)
        act = jax.nn.silu(g) * u
        routed = jnp.einsum('tei,eih,te->th', act, w_down, combine)
        sg = jax.nn.silu(x @ ws_gate) * (x @ ws_up)
        shared = sg @ ws_down
        return (routed + shared).reshape(b, s, h)

    def _L2_xattn_ref(kv, q, mask, Wq, bq, Wk, bk, Wv, bv, qn_scale, qn_bias, kn_scale, kn_bias, vn_scale, vn_bias, Wo, bo):
        import jax, jax.numpy as jnp
        import numpy as np
        D_MODEL = 256
        HEADS = 16
        D_K = D_MODEL // HEADS
        LN_EPS = 1e-06
        NEG_INF = -1000000000.0

        def _layernorm(x, scale, bias):
            mu = jnp.mean(x, axis=-1, keepdims=True)
            var = jnp.var(x, axis=-1, keepdims=True)
            return (x - mu) * jax.lax.rsqrt(var + LN_EPS) * scale + bias
        bs = q.shape[0]
        query = _layernorm(q @ Wq + bq, qn_scale, qn_bias)
        key = _layernorm(kv @ Wk + bk, kn_scale, kn_bias)
        value = _layernorm(kv @ Wv + bv, vn_scale, vn_bias)
        query = query.reshape(bs, -1, HEADS, D_K).transpose(0, 2, 1, 3)
        key = key.reshape(bs, -1, HEADS, D_K).transpose(0, 2, 1, 3)
        value = value.reshape(bs, -1, HEADS, D_K).transpose(0, 2, 1, 3)
        scores = jnp.einsum('bhqd,bhkd->bhqk', query, key) / jnp.sqrt(jnp.asarray(D_K, query.dtype))
        m = mask[:, None, :, :]
        scores = jnp.where(m == 0, NEG_INF, scores)
        probs = jax.nn.softmax(scores, axis=-1)
        out = jnp.einsum('bhqk,bhkd->bhqd', probs, value)
        out = out.transpose(0, 2, 1, 3).reshape(bs, -1, D_MODEL)
        return out @ Wo + bo

    def _L2_ffn_ref(x, w_gate, w_up, w_down):
        import jax, jax.numpy as jnp
        import numpy as np
        HIDDEN = 256
        INNER = 1024

        def _weight_quant(w):
            scale = 1.0 / jnp.clip(jnp.mean(jnp.abs(w)), 1e-05)
            wq = jnp.clip(jnp.round(w * scale), -1.0, 1.0) / scale
            return w + jax.lax.stop_gradient(wq - w)

        def _act_quant(x):
            scale = 127.0 / jnp.clip(jnp.max(jnp.abs(x), axis=-1, keepdims=True), 1e-05)
            xq = jnp.clip(jnp.round(x * scale), -128.0, 127.0) / scale
            return x + jax.lax.stop_gradient(xq - x)

        def _bitlinear(x, w):
            return jnp.einsum('bsi,oi->bso', _act_quant(x), _weight_quant(w))
        gate = jax.nn.silu(_bitlinear(x, w_gate))
        up = _bitlinear(x, w_up)
        return _bitlinear(gate * up, w_down)

    def _L3_xattn_ref(q, k, v):
        import jax, jax.numpy as jnp
        import numpy as np
        NUM_HEADS = 16
        B, S, dim = q.shape
        H = NUM_HEADS
        D = dim // H
        scale = D ** (-0.5)
        qh = q.reshape(B, S, H, D) * scale
        kh = k.reshape(B, S, H, D)
        vh = v.reshape(B, S, H, D)
        scores = jnp.einsum('bqhd,bkhd->bhqk', qh, kh)
        weights = jax.nn.softmax(scores, axis=-1)
        out = jnp.einsum('bhqk,bkhd->bqhd', weights, vh)
        return out.reshape(B, S, dim)

    def _L3_ffn_ref(x, qweights, scales, biases, lora_a, lora_b, ln_gamma, ln_beta):
        import jax, jax.numpy as jnp
        import numpy as np
        GROUP = 16
        EPS = 1e-05

        def _dequant(q, scale):
            w = q.astype(jnp.float32) / 7.5 - 1.0
            return w * jnp.repeat(scale, GROUP, axis=1)

        def _qlora_linear(x, q, scale, bias, la, lb):
            w = _dequant(q, scale)
            base = jnp.einsum('btd,od->bto', x, w) + bias
            lora = jnp.einsum('btr,or->bto', jnp.einsum('btd,rd->btr', x, la), lb)
            return base + lora

        def _layernorm(x, g, b):
            mu = jnp.mean(x, axis=-1, keepdims=True)
            var = jnp.mean(jnp.square(x - mu), axis=-1, keepdims=True)
            return (x - mu) * jax.lax.rsqrt(var + EPS) * g + b
        h = x
        for blk in range(3):
            i0, i1 = (2 * blk, 2 * blk + 1)
            y = _qlora_linear(h, qweights[i0], scales[i0], biases[i0], lora_a[i0], lora_b[i0])
            y = _layernorm(y, ln_gamma[blk], ln_beta[blk])
            y = jax.nn.gelu(y, approximate=False)
            y = _qlora_linear(y, qweights[i1], scales[i1], biases[i1], lora_a[i1], lora_b[i1])
            h = y + h
        return h
    x = x + _L0_xattn_ref(_layernorm(x, axis=-1), ctx_1024, ctx_1024, L0_xattn_Wq, L0_xattn_Wk, L0_xattn_Wv, L0_xattn_bv, L0_xattn_Wo, L0_xattn_bo)
    x = x + _L0_ffn_ref(_layernorm(x, axis=-1), L0_ffn_weight)
    x = x + _L1_xattn_ref(_layernorm(x, axis=-1), ctx_1024, ctx_1024, L1_xattn_Wq, L1_xattn_bq, L1_xattn_Wk, L1_xattn_bk, L1_xattn_Wv, L1_xattn_bv, L1_xattn_Wo, L1_xattn_bo)
    x = x + _L1_ffn_ref(_layernorm(x, axis=-1), L1_ffn_gate_w, L1_ffn_w_gate, L1_ffn_w_up, L1_ffn_w_down, L1_ffn_ws_gate, L1_ffn_ws_up, L1_ffn_ws_down)
    x = x + _L2_xattn_ref(ctx_1024, _layernorm(x, axis=-1), mask_BxSxS2_ik0, L2_xattn_Wq, L2_xattn_bq, L2_xattn_Wk, L2_xattn_bk, L2_xattn_Wv, L2_xattn_bv, L2_xattn_qn_scale, L2_xattn_qn_bias, L2_xattn_kn_scale, L2_xattn_kn_bias, L2_xattn_vn_scale, L2_xattn_vn_bias, L2_xattn_Wo, L2_xattn_bo)
    x = x + _L2_ffn_ref(_layernorm(x, axis=-1), L2_ffn_w_gate, L2_ffn_w_up, L2_ffn_w_down)
    x = x + _L3_xattn_ref(_layernorm(x, axis=-1), ctx_1024, ctx_1024)
    x = x + _L3_ffn_ref(_layernorm(x, axis=-1), L3_ffn_qweights, L3_ffn_scales, L3_ffn_biases, L3_ffn_lora_a, L3_ffn_lora_b, L3_ffn_ln_gamma, L3_ffn_ln_beta)
    return x

_drawn_inputs = setup_inputs


def setup_inputs(seed=0):
    import zlib

    import numpy as np

    out = dict(_drawn_inputs(seed))
    spreads = {'L2_xattn_bq': (0.0, 2.0),
     'L2_xattn_bk': (0.0, 2.0),
     'L2_xattn_bv': (0.0, 0.8),
     'L2_xattn_qn_scale': (1.0, 0.6),
     'L2_xattn_qn_bias': (0.0, 2.0),
     'L2_xattn_kn_scale': (1.0, 0.6),
     'L2_xattn_kn_bias': (0.0, 2.0),
     'L2_xattn_vn_scale': (1.0, 0.6),
     'L2_xattn_vn_bias': (0.0, 0.8),
     'L2_xattn_bo': (0.0, 0.8),
     'L3_ffn_ln_gamma': (1.0, 0.2),
     'L3_ffn_ln_beta': (0.0, 0.39)}
    factors = {'L1_xattn_Wq': 4.128,
     'L1_xattn_bq': 8.0,
     'L1_xattn_Wk': 4.115,
     'L1_xattn_bk': 64.0,
     'L1_xattn_bv': 8.0,
     'L1_xattn_bo': 8.0,
     'L1_ffn_gate_w': 8.0,
     'L1_ffn_w_gate': 8.0,
     'L1_ffn_w_up': 8.0,
     'L1_ffn_w_down': 8.0,
     'L1_ffn_ws_gate': 8.0,
     'L1_ffn_ws_up': 8.0,
     'L1_ffn_ws_down': 8.0,
     'L2_xattn_Wq': 3.943,
     'L2_xattn_Wk': 3.99,
     'L2_ffn_w_gate': 5.984,
     'L2_ffn_w_up': 5.768,
     'L2_ffn_w_down': 5.741,
     'L3_ffn_biases': 51.387,
     'L3_ffn_lora_a': 8.0,
     'L3_ffn_lora_b': 8.0}
    for name, (base, spread) in spreads.items():
        noise = np.random.default_rng([zlib.crc32(name.encode()), seed]).standard_normal(out[name].shape)
        drawn = base * np.exp(spread * noise) if base else spread * noise
        out[name] = jnp.asarray(drawn.astype(out[name].dtype))
    for name, factor in factors.items():
        out[name] = (out[name] * factor).astype(out[name].dtype)
    return out
```

```python
from contextlib import ExitStack

import concourse.bass as bass
from concourse import mybir

F32 = mybir.dt.float32
BF16 = mybir.dt.bfloat16
I32 = mybir.dt.int32
ALU = mybir.AluOpType
ACT = mybir.ActivationFunctionType
AX = mybir.AxisListType

P = 128
B, S, D = 8, 256, 256
KT = D // P
H, DH = 16, 16
NB = 2
STEPS = B // NB
TOK = NB * S
NT = TOK // P
SJ = S // P
E, TOP_K, INNER_E = 16, 2, 128
ES = E + 2
RING = 6
INNER = 1024
R_LORA = 32
GROUP = 16
NBLK = 3
HG = 4
HPG = H // HG
DPAD = 32
SPLIT_Q = (0, 0, 1, 0, 1, 2)
SPLIT_K = (0, 1, 0, 2, 1, 0)
NSPLIT = len(SPLIT_Q)
KROWS = NSPLIT * DH
KALL = KROWS + 2
NEG = -1e30
SCALE = DH ** -0.5
ROUND = 1.5 * 2.0 ** 23
LN_EPS = 1e-5
L2_EPS = 1e-6
CLIP = 1e-5
Q_MAX = 127.0

W_L0Q, W_L0K, W_L0V, W_L0F, W_L1Q, W_L1K, W_L1V, W_L2Q, W_L2K, W_L2V = range(10)
W_QKV = ((W_L0Q, W_L0K, W_L0V), (W_L1Q, W_L1K, W_L1V), (W_L2Q, W_L2K, W_L2V))
(V_L0BV, V_L0BO, V_L1BV, V_L1BO, V_L2BQ, V_L2BK, V_L2BV, V_L2VS, V_L2VB, V_L2BO, V_L3B) = range(11)
V_BV = (V_L0BV, V_L1BV)
V_BO = (V_L0BO, V_L1BO, V_L2BO)
N_VEC = V_L3B + 6
C_L1BQ, C_L1BK, C_QS, C_QB, C_KS, C_KB, C_G, C_BETA = 0, 1, 2, 3, 4, 5, 6, 9
N_COL = 12


class Signal:

    def __init__(self, sem, known, unit=1, head=0):
        self.sem, self.known, self.unit, self.head, self.order = sem, known, unit, head, {}

    def step(self, key):
        assert key not in self.order, key
        self.order[key] = len(self.order)
        return self.sem, self.unit

    def at(self, i, key):
        if self.known is None:
            return self.sem, 1
        done = self.unit * (self.known[key] + 1) + self.head
        return self.sem, done if i is None else i * (self.unit * len(self.known)) + done

    def before(self, i):
        assert self.head
        return self.sem, i * (self.unit * len(self.known or [0])) + self.head


def build(nc, known, x_d, ctx_t_d, ctx_d, mask_d, mask_t_d, w_d, wo_d, vec_d, col_d, gate_d,
          expert_d, wq_gate_d, wq_up_d, wq_down_d, w3_d, scale3_d, la_d, lb_d, out_d):
    made = {}
    with ExitStack() as ctx:
        def sb(name, shape, dt=F32):
            return ctx.enter_context(nc.sbuf_tensor(name, shape, dt))

        def signal(name, unit=1, head=0):
            made[name] = Signal(ctx.enter_context(nc.semaphore(name)),
                                None if known is None else known[name], unit, head)
            return made[name]

        w = sb("w", [P, 10, KT, D])
        wo = sb("wo", [P, 3, HG, D])
        vec = sb("vec", [P, N_VEC, D])
        col = sb("col", [P, N_COL, KT])
        gate_w = sb("gate_w", [P, KT, E])
        expert = sb("expert", [P, RING, 3 * D])
        wq_gate = sb("wq_gate", [P, KT, INNER], BF16)
        wq_up = sb("wq_up", [P, KT, INNER], BF16)
        wq_down = sb("wq_down", [P, INNER // P, D], BF16)
        w3 = sb("w3", [P, 2 * NBLK, KT, D])

        ident = sb("ident", [P, P])
        ident_b = sb("ident_b", [P, P], BF16)
        ones = sb("ones", [P, P])
        pick_sum = sb("pick_sum", [P, P])
        diag_s = sb("diag_s", [P, 3, P], BF16)
        diag_t = sb("diag_t", [P, 3, P], BF16)
        neg_half = sb("neg_half", [P, NT])

        x = sb("x", [P, NT, D])
        ctx_t = sb("ctx_t", [P, KT, TOK])
        ctx_n = sb("ctx_n", [P, NT, D])
        mask_s = sb("mask_s", [P, NB, SJ, S], BF16)
        mask_t = sb("mask_t", [P, NB, SJ, S], BF16)
        xn = sb("xn", [P, NT, D])
        xn_t = sb("xn_t", [P, KT, TOK])
        q_st = sb("q_st", [P, H // 2, 2, TOK], BF16)
        k_st = sb("k_st", [P, H // 2, 2, TOK], BF16)
        qf = sb("qf", [P, 2, TOK])
        parts = sb("parts", [P, 3, 2, TOK], BF16)
        v = sb("v", [P, NT, H, DPAD])
        probs = sb("probs", [P, 2 * HPG, TOK])
        o_raw = sb("o_raw", [P, TOK])
        o_inv = sb("o_inv", [P, TOK])
        o_n = sb("o_n", [P, HG, TOK])
        neg_max = sb("neg_max", [P, HG, HPG * NB * SJ])
        max_row = sb("max_row", [HPG * NB * SJ, HG, 2, P], BF16)

        bn = sb("bn", [P, NT, 6])
        mv = sb("mv", [P, NT, 2])
        var_eps = sb("var_eps", [P, NT])
        rstd = sb("rstd", [P, NT])
        logit = sb("logit", [P, NT, E])
        lneg = sb("lneg", [P, NT])
        lsum = sb("lsum", [P, NT])
        score = sb("score", [P, NT, E + 8])
        top = sb("top", [P, NT, 8])
        wanted = sb("wanted", [P, NT, 8])
        marked = sb("marked", [P, NT, E + 8])
        combine = sb("combine", [P, NT, E])
        amax = sb("amax", [P, NT])
        qscale = sb("qscale", [P, NT])
        dq_gate = sb("dq_gate", [P, NT])
        dq_up = sb("dq_up", [P, NT])
        hmax = sb("hmax", [P, NT])
        hscale = sb("hscale", [P, NT])
        dq_down = sb("dq_down", [P, NT])
        held = sb("held", [P, 1])
        wsum = sb("wsum", [P, 3])
        w_unit = sb("w_unit", [P, 3])
        w_scale = sb("w_scale", [P, 3])

        mask_int = [probs[:, 2 * n:2 * n + 2, :].bitcast(I32).rearrange("p a t -> p (a t)") for n in range(2)]
        silu_g = [probs[:, n, :] for n in range(2)]
        act_e = [probs[:, 2 + n, :] for n in range(2)]
        hid = [probs[:, 4 + 2 * n:6 + 2 * n, :].rearrange("p a t -> p (a t)") for n in range(2)]
        hid_q = [o_n[:, n, :].bitcast(BF16) for n in range(2)]
        hid_t = [o_n[:, 2 + n, :].bitcast(BF16).rearrange("p (k t) -> p k t", k=INNER // P) for n in range(2)]
        y_tok = o_n[:, 0:2, :].rearrange("p a (b d) -> p (a b) d", b=2)
        v_tok = o_n[:, 2:4, :].rearrange("p a (b d) -> p (a b) d", b=2)
        y_t = o_n[:, 2:4, :]
        h_tok = ctx_n
        xq = parts[:, 0, :, :].rearrange("p m (a d) -> p (m a) d", a=2)
        xq_t = parts[:, 1, :, :]
        raw_w = [probs[:, 0:4, :], probs[:, 4:8, :], o_n[:, :, :]]
        raw_w = [r.rearrange("p a t -> p (a t)") for r in raw_w]
        scale3 = k_st[:, :, :, :].bitcast(F32).rearrange("p h m t -> p (h m t)")[:, 0:KT * 6 * D].rearrange(
            "p (k n o) -> p k n o", k=KT, n=6)
        lora = q_st[:, :, :, :].bitcast(F32).rearrange("p h m t -> p (h m t)")
        la = lora[0:R_LORA, 0:6 * D].rearrange("r (n d) -> r n d", n=6)
        lb = lora[0:R_LORA, 6 * D:12 * D].rearrange("r (n d) -> r n d", n=6)

        ps = ctx.enter_context(nc.psum_tensor("ps", [P, 8, 512], F32))
        filled = [signal(f"filled{b}") for b in range(8)]
        drained = [signal(f"drained{b}", head=1) for b in range(8)]
        bank_of, last_in = {}, {}
        turn = [0]

        def claim(pe, i, key, bank=None):
            if bank is None:
                bank = turn[0] % 8
                turn[0] += 1
            if bank in last_in:
                pe.wait_ge(*drained[bank].at(i, last_in[bank]))
            else:
                pe.wait_ge(*drained[bank].before(i))
            last_in[bank] = key
            bank_of[key] = bank
            drained[bank].step(key)
            return ps[:, bank, :]

        def tile_of(key):
            return ps[:, bank_of[key], :]

        def tile_filled(key):
            return filled[bank_of[key]].step(key)

        def tile_drained(key):
            return drained[bank_of[key]].sem, 1

        def wait_filled(eng, i, key):
            eng.wait_ge(*filled[bank_of[key]].at(i, key))

        def wait_drained(eng, i, key):
            eng.wait_ge(*drained[bank_of[key]].at(i, key))

        load = {n: signal("load_" + n, 16) for n in (
            "w", "wo", "vec", "col", "gate", "wq_gate", "wq_up", "wq_down",
            "w3", "scale3", "la", "lb")}
        const_ready = signal("const_ready")
        wo_clear = signal("wo_clear")
        abs_sum = signal("abs_sum")
        sum_all = signal("sum_all")
        prep = signal("prep")
        lora_done = signal("lora_done")
        lora_used = signal("lora_used")

        x_in = signal("x_in", 16)
        ctx_in = signal("ctx_in", 16)
        ctxn_in = signal("ctxn_in", 16)
        mask_in = signal("mask_in", 16)
        expert_in = [signal(f"expert_in{r}", 16) for r in range(RING)]
        mask_ready = signal("mask_ready")
        x_new = signal("x_new")
        x_bias = signal("x_bias")
        ln_stats = signal("ln_stats")
        ln_moments = signal("ln_moments")
        ln_var = signal("ln_var")
        ln_rstd = signal("ln_rstd")
        ln_done = signal("ln_done")
        tok_made = signal("tok_made")
        part_hi = signal("part_hi")
        part_rest = signal("part_rest")
        part_mid = signal("part_mid")
        part_lo = signal("part_lo")
        stacked = signal("stacked", 16)
        v_ready = signal("v_ready")
        max_hi = signal("max_hi")
        max_in = signal("max_in", 16)
        pv_done = signal("pv_done")
        o_ready = signal("o_ready")
        route = signal("route")
        route_exp = signal("route_exp")
        x_part = signal("x_part")
        quant = signal("quant")
        xq_ready = signal("xq_ready")
        silu_half = signal("silu_half")
        hid_half = signal("hid_half")
        hid_ready = signal("hid_ready")
        stored = signal("stored", 16, head=16)

        block = ctx.enter_context(nc.Block())

        def layers(part):
            part.kv(0)
            part.norm("l0a")
            part.q(0)
            part.attend(0)
            part.project(0)
            part.norm("l0f")
            part.ffn0()
            part.kv(1)
            part.norm("l1a")
            part.q(1)
            part.attend(1)
            part.project(1)
            part.norm("l1f")
            part.moe()
            part.kv(2)
            part.norm("l2a")
            part.q(2)
            part.attend(2)
            part.project(2)
            part.norm("l2f")
            part.ffn2()
            part.kv(3)
            part.norm("l3a")
            part.q(3)
            part.attend(3)
            part.project(3)
            part.norm("l3f")
            part.ffn3()

        CAUSAL = (True, True, False, False)

        def h_key(n, kt):
            return ("h", n, kt) if n else ("xt", "l3f", kt)

        def diag_kind(L, j):
            return 2 if L == 1 else (1 if j == 0 else 0)

        @block.tensor
        def _(pe):
            mm = nc.tensor.matmul

            pe.wait_ge(*const_ready.at(None, "last"))
            pe.wait_ge(*abs_sum.at(None, 2))
            mm(ps[:, 0, 0:3], ones[:, :], wsum[:, :], start=True, stop=True).then_inc(*sum_all.step("all"))
            pe.wait_ge(*load["la"].at(None, 0))
            pe.wait_ge(*load["lb"].at(None, 0))
            for n in range(2 * NBLK):
                bank = 1 + n % 4
                if n >= 4:
                    pe.wait_ge(*lora_used.at(None, n - 4))
                for kt in range(KT):
                    last = mm(ps[:, bank, kt * D:(kt + 1) * D], la[:, n, kt * P:(kt + 1) * P], lb[:, n, :],
                              start=True, stop=True)
                last.then_inc(*lora_done.step(n))
            pe.wait_ge(*load["w"].at(None, 0))
            pe.wait_ge(*prep.at(None, "last"))
            pe.wait_ge(*const_ready.at(None, "k_ones"))

            with pe.Fori(0, STEPS) as i:
                def feature_out(key, m, wn, act_t):
                    t = claim(pe, i, key)
                    for kt in range(KT):
                        last = mm(t, w[:, wn, kt, m * P:(m + 1) * P], act_t[:, kt, :],
                                  start=kt == 0, stop=kt == KT - 1)
                    last.then_inc(*tile_filled(key))

                def token_out(key, weight, act_t):
                    for n in range(NT // 2):
                        t = claim(pe, i, (*key, n))
                        for a in range(2):
                            T = 2 * n + a
                            for kt in range(KT):
                                last = mm(t[:, a * D:(a + 1) * D], act_t[:, kt, T * P:(T + 1) * P], weight[:, kt, :],
                                          start=kt == 0, stop=kt == KT - 1)
                        last.then_inc(*tile_filled((*key, n)))

                def turn_tokens(key, tok):
                    for kt in range(KT):
                        t = claim(pe, i, (*key, kt))
                        for T in range(NT):
                            last = nc.tensor.transpose(t[:, T * P:(T + 1) * P], tok[:, T, kt * P:(kt + 1) * P], ident[:, :])
                        last.then_inc(*tile_filled((*key, kt)))

                class Part:
                    def kv(L):
                        if L == 0:
                            pe.wait_ge(*ctx_in.at(i, 0))
                        if L < 2:
                            for m in range(2):
                                feature_out(("k", L, m), m, W_QKV[L][1], ctx_t)
                        if L == 2:
                            token_out(("k", L), w[:, W_L2K, :, :], ctx_t)
                        if L < 3:
                            token_out(("v", L), w[:, W_QKV[L][2], :, :], ctx_t)
                        if L == 2:
                            pe.wait_ge(*ln_done.at(i, ("k", NT - 1)))
                            turn_tokens(("kt", L), y_tok)

                    def norm(p):
                        if p == "l2f":
                            return
                        pe.wait_ge(*ln_done.at(i, (p, NT - 1)))
                        turn_tokens(("xt", p), h_tok if p == "l3f" else xn)

                    def q(L):
                        if L == 3:
                            return
                        for kt in range(KT):
                            wait_drained(pe, i, ("xt", f"l{L}a", kt))
                        if L < 2:
                            for m in range(2):
                                feature_out(("q", L, m), m, W_QKV[L][0], xn_t)
                        else:
                            token_out(("q", L), w[:, W_L2Q, :, :], xn_t)
                            pe.wait_ge(*ln_done.at(i, ("q", NT - 1)))
                            turn_tokens(("qt", L), y_tok)

                    def attend(L):
                        causal = CAUSAL[L]
                        pe.wait_ge(*stacked.at(i, ("k", L, NSPLIT - 1)))
                        pe.wait_ge(*stacked.at(i, ("q", L, NSPLIT - 1)))
                        if L == 2:
                            pe.wait_ge(*mask_ready.at(i, 1))

                        def head(t, h, rows, c0, n):
                            return t[0:rows, h // 2, h % 2, c0:c0 + n]

                        def rows_for_max(hg):
                            for h4 in range(HPG):
                                h = hg * HPG + h4
                                for b in range(NB):
                                    key = ("m", L, hg, h4, b)
                                    t = claim(pe, i, key, 4 + (h4 * NB + b) % 2)
                                    for j in (range(SJ) if not causal else (1, 0)):
                                        n = S if j or not causal else P
                                        c0 = j * S if not causal else (0 if j else S)
                                        last = mm(t[:, c0:c0 + n], head(q_st, h, KROWS, b * S + j * P, P),
                                                  head(k_st, h, KROWS, b * S, n), start=True, stop=L == 3)
                                        if causal:
                                            last = mm(t[:, c0 + n - P:c0 + n], ident_b[:, :], diag_s[:, diag_kind(L, j), :],
                                                      start=False, stop=True)
                                        elif L == 2:
                                            last = mm(t[:, c0:c0 + n], ident_b[:, :], mask_s[:, b, j, :],
                                                      start=False, stop=True)
                                    last.then_inc(*tile_filled(key))

                        def turn_max(hg):
                            wait_drained(pe, i, ("m", L, hg, HPG - 1, NB - 1))
                            t = claim(pe, i, ("t", L, hg), 7)
                            nc.tensor.transpose(t[0:HPG * NB * SJ, 0:P], neg_max[:, hg, :], ident[:, :]).then_inc(
                                *tile_filled(("t", L, hg)))

                        def scores(hg, b):
                            if b == 0:
                                pe.wait_ge(*max_in.at(i, (L, hg, 1)))
                            for h4 in range(HPG):
                                h = hg * HPG + h4
                                key = ("s", L, hg, b, h4)
                                t = claim(pe, i, key, h4)
                                for j in range(SJ):
                                    skip = P if j and causal else 0
                                    n = S - skip
                                    last = mm(t[:, j * S:j * S + n], head(k_st, h, KALL, b * S + j * P, P),
                                              head(q_st, h, KALL, b * S + skip, n), start=True, stop=L == 3)
                                    if causal:
                                        last = mm(t[:, j * S:j * S + P], ident_b[:, :], diag_t[:, diag_kind(L, j), :],
                                                  start=False, stop=True)
                                    elif L == 2:
                                        last = mm(t[:, j * S:j * S + n], ident_b[:, :], mask_t[:, b, j, :],
                                                  start=False, stop=True)
                                last.then_inc(*tile_filled(key))

                        def values(hg, b):
                            u = hg * NB + b
                            if u == 0:
                                if L < 2:
                                    wait_drained(pe, i, ("v", L, NT // 2 - 1))
                                else:
                                    pe.wait_ge(*v_ready.at(i, (L, NT - 1)))
                            t = claim(pe, i, ("o", L, hg), 6) if b == 0 else tile_of(("o", L, hg))
                            for h4 in range(HPG):
                                wait_drained(pe, i, ("s", L, hg, b, h4))
                            for j in range(SJ):
                                skip = P if j and causal else 0
                                for h4 in range(HPG):
                                    last = mm(t[h4 * DPAD:(h4 + 1) * DPAD, b * S + skip:(b + 1) * S],
                                              v[:, b * SJ + j, hg * HPG + h4, :],
                                              probs[:, (u % 2) * HPG + h4, j * S:(j + 1) * S - skip],
                                              start=j == 0, stop=j == SJ - 1, tile_position=(0, h4 * DPAD),
                                              skip_group_check=True)
                            last.then_inc(*pv_done.step((L, u)))

                        def sums(hg):
                            wait_drained(pe, i, ("o", L, hg))
                            t = claim(pe, i, ("b", L, hg), 7)
                            mm(t, pick_sum[:, :], o_raw[:, :], start=True, stop=True).then_inc(*tile_filled(("b", L, hg)))

                        rows_for_max(0)
                        turn_max(0)
                        rows_for_max(1)
                        scores(0, 0)
                        for hg in range(HG):
                            scores(hg, 1)
                            if hg:
                                sums(hg - 1)
                            values(hg, 0)
                            if hg + 1 < HG:
                                turn_max(hg + 1)
                                if hg + 2 < HG:
                                    rows_for_max(hg + 2)
                                scores(hg + 1, 0)
                            values(hg, 1)
                        sums(HG - 1)

                    def project(L):
                        pe.wait_ge(*load["wo"].at(None, HPG - 1))
                        pe.wait_ge(*o_ready.at(i, (L, HG - 1)))
                        for n in range(NT // 2):
                            if L < 3:
                                t = claim(pe, i, ("wo", L, n))
                                for a in range(2):
                                    T = 2 * n + a
                                    for hg in range(HG):
                                        last = mm(t[:, a * D:(a + 1) * D], o_n[:, hg, T * P:(T + 1) * P], wo[:, L, hg, :],
                                                  start=hg == 0, stop=hg == HG - 1)
                                last.then_inc(*tile_filled(("wo", L, n)))
                            else:
                                for a in range(2):
                                    T = 2 * n + a
                                    t = claim(pe, i, ("wo", L, T))
                                    for hg in range(HG):
                                        last = nc.tensor.transpose(t[:, hg * P:(hg + 1) * P], o_n[:, hg, T * P:(T + 1) * P],
                                                                   ident[:, :])
                                    last.then_inc(*tile_filled(("wo", L, T)))

                    def ffn0():
                        for kt in range(KT):
                            wait_drained(pe, i, ("xt", "l0f", kt))
                        token_out(("f0",), w[:, W_L0F, :, :], xn_t)

                    def moe():
                        for kt in range(KT):
                            wait_drained(pe, i, ("xt", "l1f", kt))
                        pe.wait_ge(*load["gate"].at(None, 0))
                        t = claim(pe, i, "logit", 7)
                        for T in range(NT):
                            for kt in range(KT):
                                last = mm(t[:, T * E:(T + 1) * E], xn_t[:, kt, T * P:(T + 1) * P], gate_w[:, kt, :],
                                          start=kt == 0, stop=kt == KT - 1)
                        last.then_inc(*tile_filled("logit"))

                        def up(e):
                            pe.wait_ge(*expert_in[e % RING].at(i, e))
                            for name, c0, bank in (("eg", 0, e % 2), ("eu", D, 2 + e % 2)):
                                t = claim(pe, i, (name, e), bank)
                                for kt in range(KT):
                                    last = mm(t, expert[:, e % RING, c0 + kt * INNER_E:c0 + (kt + 1) * INNER_E], xn_t[:, kt, :], start=kt == 0, stop=kt == KT - 1)
                                last.then_inc(*tile_filled((name, e)))

                        def down(e):
                            wait_drained(pe, i, ("eu", e))
                            for n in range(NT // 2):
                                t = claim(pe, i, ("ed", e, n), 4 + (2 * e + n) % 4)
                                for a in range(2):
                                    T = 2 * n + a
                                    last = mm(t[:, a * D:(a + 1) * D], act_e[e % 2][:, T * P:(T + 1) * P], expert[:, e % RING, 2 * D:3 * D],
                                              start=True, stop=True)
                                last.then_inc(*tile_filled(("ed", e, n)))

                        up(0)
                        for e in range(ES):
                            if e + 1 < ES:
                                up(e + 1)
                            down(e)

                    def ffn2():
                        pe.wait_ge(*xq_ready.at(i, NT - 1))
                        for kt in range(KT):
                            t = claim(pe, i, ("xq", kt)).bitcast(BF16)
                            for T in range(NT):
                                last = nc.tensor.transpose(t[:, T * P:(T + 1) * P], xq[:, T, kt * P:(kt + 1) * P], ident_b[:, :])
                            last.then_inc(*tile_filled(("xq", kt)))
                        for kt in range(KT):
                            wait_drained(pe, i, ("xq", kt))

                        def up(T):
                            for name, weight, bank in (("hg", wq_gate, 0), ("hu", wq_up, 2)):
                                for c in range(2):
                                    t = claim(pe, i, (name, T, c), 4 * (T % 2) + bank + c)
                                    for kt in range(KT):
                                        last = mm(t, xq_t[:, kt, T * P:(T + 1) * P], weight[:, kt, c * 512:(c + 1) * 512],
                                                  start=kt == 0, stop=kt == KT - 1)
                                    last.then_inc(*tile_filled((name, T, c)))

                        def down(T):
                            pe.wait_ge(*hid_ready.at(i, T))
                            t = claim(pe, i, ("ht", T), 4 * (T % 2)).bitcast(BF16)
                            for k in range(INNER // P):
                                last = nc.tensor.transpose(t[:, k * P:(k + 1) * P], hid_q[T % 2][:, k * P:(k + 1) * P], ident_b[:, :])
                            last.then_inc(*tile_filled(("ht", T)))
                            t = claim(pe, i, ("hd", T), 4 * (T % 2) + 1)
                            wait_drained(pe, i, ("ht", T))
                            for k in range(INNER // P):
                                last = mm(t[:, 0:D], hid_t[T % 2][:, k, :], wq_down[:, k, :], start=k == 0, stop=k == INNER // P - 1)
                            last.then_inc(*tile_filled(("hd", T)))

                        up(0)
                        for T in range(NT):
                            if T + 1 < NT:
                                up(T + 1)
                            down(T)

                    def ffn3():
                        for n in range(NBLK):
                            if n:
                                wait_drained(pe, i, ("z", n - 1, NT // 2 - 1))
                                turn_tokens(("h", n), h_tok)
                            for kt in range(KT):
                                wait_drained(pe, i, h_key(n, kt))
                            token_out(("y", n), w3[:, 2 * n, :, :], xn_t)
                            pe.wait_ge(*ln_done.at(i, (("y", n), NT - 1)))
                            turn_tokens(("yt", n), xn)
                            for kt in range(KT):
                                wait_drained(pe, i, ("yt", n, kt))
                            token_out(("z", n), w3[:, 2 * n + 1, :, :], y_t)

                layers(Part)

        @block.scalar
        def _(act):
            act.wait_ge(*prep.at(None, "last"))
            act.wait_ge(*load["col"].at(None, 0))
            with act.Fori(0, STEPS) as i:
                def drain(key, out, **kw):
                    wait_filled(act, i, key)
                    nc.scalar.activation(out, tile_of(key), ACT.Identity, **kw).then_inc(*tile_drained(key))

                def split_hi(what, L, src, kw):
                    for m in range(2):
                        if m == 0 and what == "q":
                            act.wait_ge(*part_lo.at(i, ("k", L, 1)))
                            act.wait_ge(*stacked.at(i, ("k", L, NSPLIT - 1)))
                        if src is not None:
                            drain((*src, m), qf[:, m, :], **{n: col[:, c, m:m + 1] for n, c in kw.items()})
                            wait_drained(act, i, (*src, m))
                        nc.scalar.activation(parts[:, 0, m, :], qf[:, m, :] if src is not None else ctx_t[:, m, :],
                                             ACT.Copy).then_inc(*part_hi.step((what, L, m)))
                    for m in range(2):
                        act.wait_ge(*part_rest.at(i, (what, L, m)))
                        nc.scalar.activation(parts[:, 1, m, :], qf[:, m, :], ACT.Copy).then_inc(*part_mid.step((what, L, m)))

                class Part:
                    def kv(L):
                        if L == 0:
                            act.wait_ge(*ctx_in.at(i, 0))
                        split_hi("k", L, (("k", L), ("k", L), ("kt", L), None)[L],
                                 ({}, {"bias": C_L1BK}, {"scale": C_KS, "bias": C_KB}, {})[L])

                    def norm(p):
                        if p in ("l2f", "l3a"):
                            return
                        for kt in range(KT):
                            drain(("xt", p, kt), xn_t[:, kt, :])

                    def q(L):
                        split_hi("q", L, (("q", L), ("q", L), ("qt", L), ("xt", "l3a"))[L],
                                 ({}, {"bias": C_L1BQ}, {"scale": C_QS, "bias": C_QB}, {})[L])

                    def attend(L):
                        width = TOK - P if CAUSAL[L] else TOK
                        if L == 0:
                            act.wait_ge(*mask_ready.at(i, 1))

                        def exps(hg, b):
                            u = hg * NB + b
                            if u >= 2:
                                act.wait_ge(*pv_done.at(i, (L, u - 2)))
                            for h4 in range(HPG):
                                key = ("s", L, hg, b, h4)
                                wait_filled(act, i, key)
                                nc.scalar.activation(probs[:, (u % 2) * HPG + h4, 0:width], tile_of(key)[:, 0:width],
                                                     ACT.Exp, scale=SCALE).then_inc(*tile_drained(key))

                        def raw(hg):
                            act.wait_ge(*pv_done.at(i, (L, hg * NB + 1)))
                            if hg:
                                act.wait_ge(*o_ready.at(i, (L, hg - 1)))
                            nc.scalar.activation(o_raw[:, :], tile_of(("o", L, hg)), ACT.Copy).then_inc(
                                *tile_drained(("o", L, hg)))

                        for hg in range(HG):
                            exps(hg, 0)
                            if hg:
                                raw(hg - 1)
                            exps(hg, 1)
                        raw(HG - 1)

                    def project(L):
                        pass

                    def ffn0():
                        pass

                    def moe():
                        act.wait_ge(*route.at(i, "shift"))
                        nc.scalar.activation(logit[:, :, :], logit[:, :, :], ACT.Exp).then_inc(*route_exp.step(0))
                        for e in range(ES):
                            wait_filled(act, i, ("eg", e))
                            if e >= 2:
                                wait_drained(act, i, ("eu", e - 2))
                            nc.scalar.activation(silu_g[e % 2], tile_of(("eg", e)), ACT.Silu).then_inc(*tile_drained(("eg", e)))

                    def ffn2():
                        for kt in range(KT):
                            wait_filled(act, i, ("xq", kt))
                            nc.scalar.activation(xq_t[:, kt, :], tile_of(("xq", kt)).bitcast(BF16)[:, 0:TOK],
                                                 ACT.Copy).then_inc(*tile_drained(("xq", kt)))

                        def gate(T):
                            if T >= 2:
                                act.wait_ge(*hid_ready.at(i, T - 2))
                            for c in range(2):
                                wait_filled(act, i, ("hg", T, c))
                                nc.scalar.activation(hid[T % 2][:, c * 512:(c + 1) * 512], tile_of(("hg", T, c)), ACT.Silu,
                                                     scale=dq_gate[:, T:T + 1]).then_inc(*tile_drained(("hg", T, c)))

                        act.wait_ge(*quant.at(i, "dq_gate"))
                        gate(0)
                        for T in range(NT):
                            if T + 1 < NT:
                                gate(T + 1)
                            wait_filled(act, i, ("ht", T))
                            nc.scalar.activation(hid_t[T % 2], tile_of(("ht", T)).bitcast(BF16).rearrange(
                                "p (k t) -> p k t", k=INNER // P), ACT.Copy).then_inc(*tile_drained(("ht", T)))

                    def ffn3():
                        for n in range(NBLK):
                            if n:
                                for kt in range(KT):
                                    drain(("h", n, kt), xn_t[:, kt, :])
                            for kt in range(KT):
                                wait_filled(act, i, ("yt", n, kt))
                                nc.scalar.activation(y_t[:, kt, :], tile_of(("yt", n, kt)), ACT.Gelu,
                                                     scale=col[:, C_G + n, kt:kt + 1],
                                                     bias=col[:, C_BETA + n, kt:kt + 1]).then_inc(*tile_drained(("yt", n, kt)))

                layers(Part)

        @block.vector
        def _(dve):
            V = nc.vector

            for n, name in enumerate(("wq_gate", "wq_up", "wq_down")):
                dve.wait_ge(*load[name].at(None, 0))
                V.tensor_reduce(wsum[:, n:n + 1], raw_w[n], AX.X, ALU.add, apply_absolute_value=True).then_inc(*abs_sum.step(n))
            dve.wait_ge(*sum_all.at(None, "all"))
            V.tensor_scalar(w_unit[:, :], ps[:, 0, 0:3], 1.0 / (D * INNER), CLIP, ALU.mult, ALU.max).then_inc(*prep.step("unit"))
            dve.wait_ge(*prep.at(None, "unit"))
            V.reciprocal(w_scale[:, :], w_unit[:, :]).then_inc(*prep.step("scale"))
            dve.wait_ge(*prep.at(None, "scale"))
            flat = [t[:, :, :].rearrange("p a b -> p (a b)") for t in (wq_gate, wq_up, wq_down)]
            for n in range(3):
                V.tensor_scalar(raw_w[n], raw_w[n], w_scale[:, n:n + 1], ROUND, ALU.mult, ALU.add).then_inc(*prep.step(("round", n)))
            for n in range(3):
                dve.wait_ge(*prep.at(None, ("round", n)))
                V.tensor_scalar(raw_w[n], raw_w[n], ROUND, 1.0, ALU.subtract, ALU.min).then_inc(*prep.step(("min", n)))
            for n in range(3):
                dve.wait_ge(*prep.at(None, ("min", n)))
                V.tensor_scalar(flat[n], raw_w[n], -1.0, None, ALU.max).then_inc(*prep.step(("max", n)))
            dve.wait_ge(*load["w"].at(None, 0))
            sign = w[:, W_L0F, :, :].rearrange("p k n -> p (k n)")
            below = xn[:, 0:2, :].rearrange("p a d -> p (a d)")
            V.tensor_scalar(below, sign, 0.0, None, ALU.is_lt).then_inc(*prep.step("below"))
            dve.wait_ge(*prep.at(None, "below"))
            V.scalar_tensor_tensor(sign, sign, 0.0, below, ALU.is_gt, ALU.subtract).then_inc(*prep.step("sign"))
            dve.wait_ge(*load["w3"].at(None, 0))
            dve.wait_ge(*load["scale3"].at(None, KT - 1))
            for n in range(2 * NBLK):
                V.tensor_scalar(w3[:, n, :, :], w3[:, n, :, :].bitcast(I32), 1.0 / 7.5, -1.0, ALU.mult, ALU.add).then_inc(
                    *prep.step(("deq", n)))
            for n in range(2 * NBLK):
                dve.wait_ge(*prep.at(None, ("deq", n)))
                V.tensor_tensor(w3[:, n, :, :], w3[:, n, :, :], scale3[:, :, n, :], ALU.mult).then_inc(*prep.step(("mul", n)))
            for n in range(2 * NBLK):
                dve.wait_ge(*prep.at(None, ("mul", n)))
                dve.wait_ge(*lora_done.at(None, n))
                V.tensor_tensor(w3[:, n, :, :], ps[:, 1 + n % 4, :].rearrange("p (k o) -> p k o", k=KT), w3[:, n, :, :],
                                ALU.add).then_inc(*lora_used.step(n))
            dve.wait_ge(*lora_used.at(None, 2 * NBLK - 1))
            dve.wait_ge(*const_ready.at(None, "last"))
            V.memset(wsum[:, :], 0.0).then_inc(*prep.step("last"))
            dve.wait_ge(*prep.at(None, "last"))
            for bank in drained:
                dve.sem_inc(bank.sem, bank.head)
            dve.wait_ge(*load["vec"].at(None, 0))

            with dve.Fori(0, STEPS) as i:
                def hold():
                    V.tensor_copy(held[:, :], neg_half[:, 0:1])

                def spread(n, many):
                    return vec[:, n, :].unsqueeze(1).to_broadcast([P, many, D])

                def layer_norm(key, src, dst, eps, wait_src, heads_last=False):
                    for T in range(NT):
                        wait_src(T)
                        V.bn_stats(bn[:, T, :], src[:, T, :]).then_inc(*ln_stats.step((key, T)))
                    dve.wait_ge(*ln_stats.at(i, (key, NT - 1)))
                    hold()
                    for T in range(NT):
                        V.bn_aggr(mv[:, T, :], bn[:, T, :]).then_inc(*ln_moments.step((key, T)))
                    dve.wait_ge(*ln_moments.at(i, (key, NT - 1)))
                    V.tensor_scalar(var_eps[:, :], mv[:, :, 1], eps, None, ALU.add).then_inc(*ln_var.step(key))
                    dve.wait_ge(*ln_rstd.at(i, key))
                    for T in range(NT):
                        out, inp = dst[:, T, :], src[:, T, :]
                        if heads_last:
                            out = out.rearrange("p (m d h) -> p h m d", m=2, d=DH)
                            inp = inp.rearrange("p (h m d) -> p h m d", m=2, d=DH)
                        V.tensor_scalar(out, inp, mv[:, T, 0:1], rstd[:, T:T + 1], ALU.subtract, ALU.mult).then_inc(
                            *ln_done.step((key, T)))

                def with_bias(key, n_vec, dst):
                    for n in range(NT // 2):
                        wait_filled(dve, i, (*key, n))
                        V.tensor_tensor(dst[:, 2 * n:2 * n + 2, :], tile_of((*key, n)).rearrange("p (a d) -> p a d", a=2),
                                        spread(n_vec, 2), ALU.add).then_inc(*tile_drained((*key, n)))

                def split_rest(what, L):
                    for m in range(2):
                        dve.wait_ge(*part_hi.at(i, (what, L, m)))
                        src = ctx_t if (what, L) == ("k", 3) else qf
                        V.tensor_tensor(qf[:, m, :], src[:, m, :], parts[:, 0, m, :], ALU.subtract).then_inc(
                            *part_rest.step((what, L, m)))

                def add_pairs(key, stage, out=x, base=x):
                    for n in range(NT // 2):
                        wait_filled(dve, i, (*key, n))
                        for a in range(2):
                            T = 2 * n + a
                            V.tensor_tensor(out[:, T, :], tile_of((*key, n))[:, a * D:(a + 1) * D], base[:, T, :], ALU.add).then_inc(
                                *(x_new.step((*stage, T)) if a == 0 else tile_drained((*key, n))))

                def wait_pairs(key, stage, T):
                    if T % 2 == 0:
                        dve.wait_ge(*x_new.at(i, (*stage, T)))
                    else:
                        wait_drained(dve, i, (*key, T // 2))

                def x_ready(p, T):
                    if p == "l0a":
                        dve.wait_ge(*x_in.at(i, 0))
                    elif p in ("l0f", "l1f", "l2f"):
                        wait_pairs(("wo", "l012".index(p[1]) - 1), ("wo", int(p[1])), T)
                    elif p == "l1a":
                        wait_pairs(("f0",), ("f0",), T)
                    elif p == "l2a":
                        e = ES - 1
                        if T % 2 == 0:
                            dve.wait_ge(*x_part.at(i, (e, T)))
                        else:
                            wait_drained(dve, i, ("ed", e, T // 2))
                    elif p == "l3a":
                        wait_drained(dve, i, ("hd", T))
                    elif p == "l3f":
                        wait_drained(dve, i, ("wo", 3, T))

                class Part:
                    def kv(L):
                        Part.norm_now(f"l{L}a")
                        if L == 2:
                            with_bias(("k", L), V_L2BK, y_tok)
                            layer_norm("k", y_tok, y_tok, L2_EPS, lambda T: wait_drained(dve, i, ("k", L, T // 2)))
                            with_bias(("v", L), V_L2BV, v_tok)
                            layer_norm("v", v_tok, v_tok, L2_EPS, lambda T: wait_drained(dve, i, ("v", L, T // 2)))
                            for T in range(NT):
                                dve.wait_ge(*ln_done.at(i, ("v", T)))
                                V.tensor_tensor(v_tok[:, T, :], v_tok[:, T, :], vec[:, V_L2VS, :], ALU.mult).then_inc(
                                    *tok_made.step(("v", T)))
                            for T in range(NT):
                                dve.wait_ge(*tok_made.at(i, ("v", T)))
                                V.tensor_tensor(v[:, T, :, 0:DH], v_tok[:, T, :].rearrange("p (h d) -> p h d", d=DH),
                                                vec[:, V_L2VB, :].rearrange("p (h d) -> p h d", d=DH), ALU.add).then_inc(
                                    *v_ready.step((L, T)))
                        if L == 3:
                            dve.wait_ge(*ctxn_in.at(i, 0))
                            for T in range(NT):
                                V.tensor_copy(v[:, T, :, 0:DH], ctx_n[:, T, :].rearrange("p (h d) -> p h d", d=DH)).then_inc(
                                    *v_ready.step((L, T)))
                        split_rest("k", L)
                        if L == 0:
                            dve.wait_ge(*mask_in.at(i, 1))
                            for n, out in enumerate((mask_s, mask_t)):
                                V.tensor_scalar(out[:, :, :, :].rearrange("p b j t -> p (b j t)"), mask_int[n], 0, NEG,
                                                ALU.is_equal, ALU.mult).then_inc(*mask_ready.step(n))
                        if L < 2:
                            for n in range(NT // 2):
                                wait_filled(dve, i, ("v", L, n))
                                for a in range(2):
                                    T = 2 * n + a
                                    done = V.tensor_tensor(
                                        v[:, T, :, 0:DH],
                                        tile_of(("v", L, n))[:, a * D:(a + 1) * D].rearrange("p (h d) -> p h d", d=DH),
                                        vec[:, V_BV[L], :].rearrange("p (h d) -> p h d", d=DH), ALU.add)
                                done.then_inc(*tile_drained(("v", L, n)))

                    def norm_now(p):
                        layer_norm(p, x, h_tok if p == "l3f" else xn, LN_EPS, lambda T: x_ready(p, T), heads_last=p == "l3a")

                    def norm(p):
                        if not p.endswith("a"):
                            Part.norm_now(p)

                    def q(L):
                        if L == 2:
                            with_bias(("q", L), V_L2BQ, y_tok)
                            layer_norm("q", y_tok, y_tok, L2_EPS, lambda T: wait_drained(dve, i, ("q", L, T // 2)))
                        split_rest("q", L)

                    def attend(L):
                        causal = CAUSAL[L]

                        def maxima(hg):
                            for h4 in range(HPG):
                                for b in range(NB):
                                    key = ("m", L, hg, h4, b)
                                    wait_filled(dve, i, key)
                                    c = (h4 * NB + b) * SJ
                                    last_key = h4 == HPG - 1 and b == NB - 1
                                    if causal:
                                        V.tensor_reduce(neg_max[:, hg, c + 1:c + 2], tile_of(key)[:, 0:S], AX.X, ALU.max, negate=True)
                                        done = V.tensor_reduce(neg_max[:, hg, c:c + 1], tile_of(key)[:, S:S + P], AX.X, ALU.max, negate=True)
                                    else:
                                        done = V.tensor_reduce(neg_max[:, hg, c:c + 2], tile_of(key).rearrange("p (j t) -> p j t", j=SJ),
                                                               AX.X, ALU.max, negate=True)
                                    done.then_inc(*tile_drained(key))

                        def max_rows(hg):
                            key = ("t", L, hg)
                            wait_filled(dve, i, key)
                            t = tile_of(key)[0:HPG * NB * SJ, 0:P]
                            V.tensor_copy(max_row[:, hg, 0, :], t).then_inc(*max_hi.step((L, hg)))
                            dve.wait_ge(*max_hi.at(i, (L, hg)))
                            V.tensor_tensor(max_row[:, hg, 1, :], t, max_row[:, hg, 0, :], ALU.subtract).then_inc(*tile_drained(key))

                        def invert(hg):
                            wait_filled(dve, i, ("b", L, hg))
                            if hg:
                                dve.wait_ge(*o_ready.at(i, (L, hg - 1)))
                            V.reciprocal(o_inv[:, :], tile_of(("b", L, hg))).then_inc(*tile_drained(("b", L, hg)))

                        maxima(0)
                        max_rows(0)
                        maxima(1)
                        for hg in range(HG):
                            if hg:
                                invert(hg - 1)
                            if hg + 1 < HG:
                                max_rows(hg + 1)
                                if hg + 2 < HG:
                                    maxima(hg + 2)
                        invert(HG - 1)

                    def project(L):
                        if L < 3:
                            dve.wait_ge(*x_bias.at(i, (L, NT - 1)))
                            add_pairs(("wo", L), ("wo", L))
                            return
                        for T in range(NT):
                            wait_filled(dve, i, ("wo", L, T))
                            V.tensor_tensor(x[:, T, :].rearrange("p (h d) -> p h d", d=DH),
                                            tile_of(("wo", L, T)).rearrange("p (h e) -> p h e", e=DPAD)[:, :, 0:DH],
                                            x[:, T, :].rearrange("p (h d) -> p h d", d=DH), ALU.add).then_inc(
                                *tile_drained(("wo", L, T)))

                    def ffn0():
                        add_pairs(("f0",), ("f0",))

                    def moe():
                        wait_filled(dve, i, "logit")
                        V.tensor_copy(logit[:, :, :], tile_of("logit")[:, 0:NT * E].rearrange("p (t e) -> p t e", e=E)).then_inc(
                            *tile_drained("logit"))
                        wait_drained(dve, i, "logit")
                        V.tensor_reduce(lneg[:, :], logit[:, :, :], AX.X, ALU.max).then_inc(*route.step("max"))
                        dve.wait_ge(*route.at(i, "max"))
                        V.tensor_tensor(logit[:, :, :], logit[:, :, :], lneg[:, :].unsqueeze(2).to_broadcast([P, NT, E]),
                                        ALU.subtract).then_inc(*route.step("shift"))
                        dve.wait_ge(*route_exp.at(i, 0))
                        V.tensor_reduce(lsum[:, :], logit[:, :, :], AX.X, ALU.add).then_inc(*route.step("sum"))
                        dve.wait_ge(*route.at(i, "sum"))
                        V.reciprocal(lsum[:, :], lsum[:, :]).then_inc(*route.step("inverse"))
                        dve.wait_ge(*route.at(i, "inverse"))
                        V.tensor_tensor(score[:, :, 0:E], logit[:, :, :], lsum[:, :].unsqueeze(2).to_broadcast([P, NT, E]),
                                        ALU.mult).then_inc(*route.step("score"))
                        dve.wait_ge(*route.at(i, "score"))
                        hold()
                        for T in range(NT):
                            V.max(top[:, T, :], score[:, T, 0:E]).then_inc(*route.step(("top", T)))
                        dve.wait_ge(*route.at(i, ("top", NT - 1)))
                        V.tensor_copy(wanted[:, :, 0:TOP_K], top[:, :, 0:TOP_K]).then_inc(*route.step("wanted"))
                        dve.wait_ge(*route.at(i, "wanted"))
                        hold()
                        for T in range(NT):
                            V.match_replace(marked[:, T, :], wanted[:, T, :], score[:, T, :], 2.0).then_inc(*route.step(("mark", T)))
                        dve.wait_ge(*route.at(i, ("mark", NT - 1)))
                        V.scalar_tensor_tensor(combine[:, :, :], marked[:, :, 0:E], 1.5, score[:, :, 0:E], ALU.is_ge,
                                               ALU.mult).then_inc(*route.step("combine"))
                        dve.wait_ge(*route.at(i, "combine"))

                        def gated(e):
                            wait_drained(dve, i, ("eg", e))
                            wait_filled(dve, i, ("eu", e))
                            V.tensor_tensor(act_e[e % 2], tile_of(("eu", e)), silu_g[e % 2], ALU.mult).then_inc(*tile_drained(("eu", e)))

                        def gather(e):
                            for n in range(NT // 2):
                                wait_filled(dve, i, ("ed", e, n))
                                for a in range(2):
                                    T = 2 * n + a
                                    if e == 0:
                                        dve.wait_ge(*ln_done.at(i, ("l1f", T)))
                                    elif a == 0:
                                        dve.wait_ge(*x_part.at(i, (e - 1, T)))
                                    else:
                                        wait_drained(dve, i, ("ed", e - 1, n))
                                    part = tile_of(("ed", e, n))[:, a * D:(a + 1) * D]
                                    if e < E:
                                        done = V.scalar_tensor_tensor(x[:, T, :], part, combine[:, T, e:e + 1], x[:, T, :],
                                                                      ALU.mult, ALU.add)
                                    else:
                                        done = V.tensor_tensor(x[:, T, :], part, x[:, T, :], ALU.add)
                                    done.then_inc(*(x_part.step((e, T)) if a == 0 else tile_drained(("ed", e, n))))

                        gated(0)
                        for e in range(ES):
                            if e + 1 < ES:
                                gated(e + 1)
                            gather(e)

                    def ffn2():
                        dve.wait_ge(*ln_done.at(i, ("l2f", NT - 1)))
                        V.tensor_reduce(amax[:, :], xn[:, :, :], AX.X, ALU.max, apply_absolute_value=True).then_inc(*quant.step("amax"))
                        dve.wait_ge(*quant.at(i, "amax"))
                        V.tensor_scalar(amax[:, :], amax[:, :], CLIP, 1.0 / Q_MAX, ALU.max, ALU.mult).then_inc(*quant.step("clip"))
                        dve.wait_ge(*quant.at(i, "clip"))
                        V.reciprocal(qscale[:, :], amax[:, :]).then_inc(*quant.step("scale"))
                        V.tensor_scalar(dq_up[:, :], amax[:, :], w_unit[:, 1:2], None, ALU.mult).then_inc(*quant.step("dq_up"))
                        V.tensor_scalar(dq_gate[:, :], amax[:, :], w_unit[:, 0:1], None, ALU.mult).then_inc(*quant.step("dq_gate"))
                        dve.wait_ge(*quant.at(i, "dq_gate"))
                        for T in range(NT):
                            V.tensor_scalar(xn[:, T, :], xn[:, T, :], qscale[:, T:T + 1], ROUND, ALU.mult, ALU.add).then_inc(
                                *quant.step(("round", T)))
                        for T in range(NT):
                            dve.wait_ge(*quant.at(i, ("round", T)))
                            V.tensor_scalar(xq[:, T, :], xn[:, T, :], ROUND, Q_MAX, ALU.subtract, ALU.min).then_inc(*xq_ready.step(T))

                        def hidden(T):
                            h = hid[T % 2]
                            for c in range(2):
                                wait_drained(dve, i, ("hg", T, c))
                                wait_filled(dve, i, ("hu", T, c))
                                cs = h[:, c * 512:(c + 1) * 512]
                                V.scalar_tensor_tensor(cs, tile_of(("hu", T, c)), dq_up[:, T:T + 1], cs, ALU.mult, ALU.mult).then_inc(
                                    *tile_drained(("hu", T, c)))
                            for c in range(2):
                                wait_drained(dve, i, ("hu", T, c))
                            hm = hmax[:, T:T + 1]
                            V.tensor_reduce(hm, h, AX.X, ALU.max, apply_absolute_value=True).then_inc(*quant.step(("hmax", T)))
                            dve.wait_ge(*quant.at(i, ("hmax", T)))
                            V.tensor_scalar(hm, hm, CLIP, 1.0 / Q_MAX, ALU.max, ALU.mult).then_inc(*quant.step(("hclip", T)))
                            dve.wait_ge(*quant.at(i, ("hclip", T)))
                            V.reciprocal(hscale[:, T:T + 1], hm).then_inc(*quant.step(("hscale", T)))
                            V.tensor_scalar(dq_down[:, T:T + 1], hm, w_unit[:, 2:3], None, ALU.mult).then_inc(*quant.step(("dqd", T)))
                            dve.wait_ge(*quant.at(i, ("dqd", T)))
                            V.tensor_scalar(h, h, hscale[:, T:T + 1], ROUND, ALU.mult, ALU.add).then_inc(*quant.step(("hround", T)))
                            dve.wait_ge(*quant.at(i, ("hround", T)))
                            if T >= 2:
                                wait_filled(dve, i, ("ht", T - 2))
                            V.tensor_scalar(hid_q[T % 2], h, ROUND, Q_MAX, ALU.subtract, ALU.min).then_inc(*hid_ready.step(T))

                        def gather(T):
                            wait_filled(dve, i, ("hd", T))
                            V.scalar_tensor_tensor(x[:, T, :], tile_of(("hd", T))[:, 0:D], dq_down[:, T:T + 1], x[:, T, :],
                                                   ALU.mult, ALU.add).then_inc(*tile_drained(("hd", T)))

                        hidden(0)
                        for T in range(NT):
                            if T + 1 < NT:
                                hidden(T + 1)
                            gather(T)

                    def ffn3():
                        for n in range(NBLK):
                            with_bias(("y", n), V_L3B + 2 * n, y_tok)
                            layer_norm(("y", n), y_tok, xn, LN_EPS, lambda T: wait_drained(dve, i, ("y", n, T // 2)))
                            dve.wait_ge(*x_bias.at(i, ("f3", n)))
                            if n < NBLK - 1:
                                add_pairs(("z", n), ("z", n), h_tok, h_tok)
                            else:
                                dve.wait_ge(*x_bias.at(i, "out"))
                                add_pairs(("z", n), ("z", n), x, h_tok)
                layers(Part)

        @block.gpsimd
        def _(pool):
            G = nc.gpsimd

            def clear(key, out, value=0.0):
                G.memset(out, value).then_inc(*const_ready.step(key))

            def select(key, after, out, pattern, base, mult, op, fill):
                pool.wait_ge(*const_ready.at(None, after))
                G.affine_select(out=out, in_=out, compare_op=op, fill=fill, base=base, pattern=pattern,
                                channel_multiplier=mult).then_inc(*const_ready.step(key))

            G.memset(wo[:, :, :, :], 0.0).then_inc(*wo_clear.step(0))
            for name, out, value in (("ident", ident[:, :], 0.0), ("ident_b", ident_b[:, :], 0.0), ("pick", pick_sum[:, :], 0.0),
                                     ("ds", diag_s[:, :, :], 0.0), ("dt", diag_t[:, :, :], 0.0), ("v", v[:, :, :, :], 0.0),
                                     ("ones", ones[:, :], 1.0), ("half", neg_half[:, :], -0.5),
                                     ("wanted", wanted[:, :, TOP_K:8], -1.0), ("score", score[:, :, E:E + 8], -1.0)):
                clear(name, out, value)
            select("ident1", "score", ident[:, :], [[-1, P]], 0, 1, ALU.not_equal, 1.0)
            select("ident_b1", "score", ident_b[:, :], [[-1, P]], 0, 1, ALU.not_equal, 1.0)
            select("pick1", "score", pick_sum[:, :].rearrange("p (g c) -> p g c", g=HPG), [[-DPAD, HPG], [0, DPAD]], -DH, 1,
                   ALU.not_equal, 1.0)
            for kind in range(3):
                strict = 0 if kind == 2 else -1
                select(("ds", kind), "score", diag_s[:, kind, :], [[-1, P]], strict, 1, ALU.is_ge, NEG)
                select(("dt", kind), "score", diag_t[:, kind, :], [[1, P]], strict, -1, ALU.is_ge, NEG)
            pool.wait_ge(*const_ready.at(None, ("dt", 2)))
            clear("open_s", diag_s[0:1, 1, 0:1])
            clear("open_t", diag_t[0:1, 1, 0:1])
            clear("last", v[:, :, :, DH:DH + 1], 1.0)
            pool.wait_ge(*prep.at(None, "last"))
            clear("k_ones", k_st[KROWS:KALL, :, :, :], 1.0)
            pool.wait_ge(*const_ready.at(None, "k_ones"))
            pool.wait_ge(*load["vec"].at(None, 0))

            with pool.Fori(0, STEPS) as i:
                def power(key):
                    pool.wait_ge(*ln_var.at(i, key))
                    G.tensor_tensor(rstd[:, :], var_eps[:, :], neg_half[:, :], ALU.pow).then_inc(*ln_rstd.step(key))

                def split_low(what, L):
                    for m in range(2):
                        pool.wait_ge(*part_mid.at(i, (what, L, m)))
                        G.tensor_tensor(parts[:, 2, m, :], qf[:, m, :], parts[:, 1, m, :], ALU.subtract).then_inc(
                            *part_lo.step((what, L, m)))

                class Part:
                    def kv(L):
                        power(f"l{L}a")
                        if L < 3:
                            for T in range(NT):
                                pool.wait_ge(*ln_done.at(i, (f"l{L}a", T)))
                                G.tensor_tensor(x[:, T, :], x[:, T, :], vec[:, V_BO[L], :], ALU.add).then_inc(*x_bias.step((L, T)))
                        if L == 2:
                            power("k")
                            power("v")
                        split_low("k", L)

                    def norm(p):
                        if not p.endswith("a"):
                            power(p)

                    def q(L):
                        if L == 2:
                            power("q")
                        split_low("q", L)

                    def attend(L):
                        for hg in range(HG):
                            wait_drained(pool, i, ("b", L, hg))
                            G.tensor_tensor(o_n[:, hg, :], o_raw[:, :], o_inv[:, :], ALU.mult).then_inc(*o_ready.step((L, hg)))

                    def project(L):
                        pass

                    ffn0 = moe = ffn2 = lambda: None

                    def ffn3():
                        for n in range(NBLK):
                            for kt in range(KT):
                                wait_drained(pool, i, h_key(n, kt))
                            G.tensor_tensor(h_tok[:, :, :], h_tok[:, :, :], vec[:, V_L3B + 2 * n + 1, :].unsqueeze(1).to_broadcast([P, NT, D]),
                                            ALU.add).then_inc(*x_bias.step(("f3", n)))
                            if n == NBLK - 1:
                                pool.wait_ge(*x_bias.at(i, ("f3", n)))
                                G.tensor_tensor(h_tok[:, :, :], h_tok[:, :, :], x[:, :, :], ALU.add).then_inc(*x_bias.step("out"))
                            power(("y", n))

                layers(Part)

        @block.sync
        def _(sp):
            sp.dma_start(la, la_d).then_inc(*load["la"].step(0))
            sp.dma_start(lb, lb_d).then_inc(*load["lb"].step(0))
            for name, out, src in (("wq_gate", raw_w[0], wq_gate_d), ("wq_up", raw_w[1], wq_up_d), ("wq_down", raw_w[2], wq_down_d),
                                   ("w", w[:, :, :, :].rearrange("p n k o -> p (n k o)"), w_d),
                                   ("w3", w3[:, :, :, :].bitcast(I32).rearrange("p n k o -> p (n k o)"), w3_d)):
                sp.dma_start(out, src).then_inc(*load[name].step(0))
            for kt in range(KT):
                sp.dma_start(scale3[:, kt, :, :].rearrange("p n o -> p (n o)"),
                             scale3_d[kt].unsqueeze(1).to_broadcast([P // GROUP, GROUP, 6 * D])).then_inc(*load["scale3"].step(kt))
            sp.dma_start(vec[:, :, :], vec_d.unsqueeze(0).to_broadcast([P, N_VEC, D])).then_inc(*load["vec"].step(0))
            sp.dma_start(col[:, :, :].rearrange("p n k -> p (n k)"), col_d).then_inc(*load["col"].step(0))
            sp.wait_ge(*wo_clear.at(None, 0))
            for g in range(HPG):
                sp.dma_start(wo[g * DPAD:g * DPAD + DH, :, :, :].rearrange("p n g o -> p (n g o)"), wo_d[g]).then_inc(
                    *load["wo"].step(g))
            sp.dma_start(gate_w[:, :, :].rearrange("p a b -> p (a b)"), gate_d).then_inc(*load["gate"].step(0))
            sp.wait_ge(*prep.at(None, "last"))
            sp.sem_inc(stored.sem, stored.head)

            with sp.Fori(0, STEPS) as i:
                def stack(what, L, st, split):
                    n = 0
                    for part, ready in enumerate((part_hi, part_mid, part_lo)):
                        sp.wait_ge(*ready.at(i, (what, L, 1)))
                        for at in range(NSPLIT):
                            if split[at] == part:
                                sp.dma_start(st[at * DH:(at + 1) * DH, :, :, :].rearrange("d h m t -> d (h m t)"),
                                             parts[:, part, :, :].rearrange("p m t -> p (m t)")).then_inc(*stacked.step((what, L, n)))
                                n += 1

                def load_expert(e):
                    sp.dma_start(expert[:, e % RING, :], expert_d[:, e, :]).then_inc(*expert_in[e % RING].step(e))

                class Part:
                    def kv(L):
                        if L == 0:
                            sp.wait_ge(*stored.before(i))
                            sp.dma_start(x[:, :, :], x_d[i]).then_inc(*x_in.step(0))
                            sp.dma_start(ctx_t[:, :, :].rearrange("p k t -> p (k t)"), ctx_t_d[i]).then_inc(*ctx_in.step(0))
                            for n, src in enumerate((mask_d, mask_t_d)):
                                sp.dma_start(mask_int[n], src[i]).then_inc(*mask_in.step(n))
                            sp.dma_start(ctx_n[:, :, :], ctx_d[i]).then_inc(*ctxn_in.step(0))
                            for e in range(RING):
                                load_expert(e)
                        stack("k", L, k_st, SPLIT_K)

                    def norm(p):
                        pass

                    def q(L):
                        stack("q", L, q_st, SPLIT_Q)

                    def attend(L):
                        for hg in range(HG):
                            wait_drained(sp, i, ("t", L, hg))
                            for n in range(2):
                                sp.dma_start(q_st[KROWS + n:KROWS + n + 1, 2 * hg:2 * hg + 2, :, :].rearrange("r h m t -> r (h m t)"),
                                             max_row[:, hg, n, :]).then_inc(*max_in.step((L, hg, n)))

                    def project(L):
                        pass

                    def moe():
                        for e in range(RING, ES):
                            wait_filled(sp, i, ("ed", e - RING, NT // 2 - 1))
                            load_expert(e)

                    ffn0 = ffn2 = lambda: None

                    def ffn3():
                        wait_drained(sp, i, ("z", NBLK - 1, NT // 2 - 1))
                        sp.dma_start(out_d[i], x[:, :, :]).then_inc(*stored.step(0))

                layers(Part)
            sp.wait_ge(stored.sem, stored.head + stored.unit * STEPS)

    return {n: s.order for n, s in made.items()}


def heads_inside(a, axis):
    import numpy as np

    shape = a.shape
    a = a.reshape(*shape[:axis], H // 2, 2, DH, *shape[axis + 1:])
    return np.ascontiguousarray(np.moveaxis(a, axis, axis + 2)).reshape(shape)


def lay_out(t):
    import numpy as np

    t = {n: np.asarray(a) for n, a in t.items()}

    def rows(a):
        return a.reshape(-1, P, a.shape[1]).transpose(1, 0, 2).reshape(P, -1)

    def steps(a):
        return a.reshape(STEPS, NB, SJ, P, -1).transpose(0, 3, 1, 2, 4).reshape(STEPS, P, -1)

    def perm(a):
        return heads_inside(a, a.ndim - 1)

    def qk(a):
        return perm(a)

    w_list = []
    for pre, turn in (("L0", True), ("L1", True), ("L2", False)):
        wq, wk, wv = (t[f"{pre}_xattn_{n}"].T if turn else t[f"{pre}_xattn_{n}"] for n in ("Wq", "Wk", "Wv"))
        w_list += [perm(wq), heads_inside(perm(wk), 0), heads_inside(wv, 0)]
        if pre == "L0":
            w_list.append(t["L0_ffn_weight"].T)
    w = np.concatenate([rows(a) for a in w_list], axis=1)
    wo = np.stack([t["L0_xattn_Wo"].T, t["L1_xattn_Wo"].T, t["L2_xattn_Wo"]])
    wo = wo.reshape(3, HG, HPG, DH, D).transpose(2, 3, 0, 1, 4).reshape(HPG, DH, -1)
    vec = np.stack([t["L0_xattn_bv"], t["L0_xattn_bo"], t["L1_xattn_bv"], t["L1_xattn_bo"], perm(t["L2_xattn_bq"]),
                    perm(t["L2_xattn_bk"]), t["L2_xattn_bv"], t["L2_xattn_vn_scale"], t["L2_xattn_vn_bias"],
                    t["L2_xattn_bo"], *t["L3_ffn_biases"]])
    col = np.stack([*(perm(t[n]) for n in ("L1_xattn_bq", "L1_xattn_bk", "L2_xattn_qn_scale", "L2_xattn_qn_bias",
                                           "L2_xattn_kn_scale", "L2_xattn_kn_bias")), *t["L3_ffn_ln_gamma"], *t["L3_ffn_ln_beta"]])
    col = col.reshape(N_COL, KT, P).transpose(2, 0, 1).reshape(P, -1)

    def experts(name):
        shared = t[f"L1_ffn_ws_{name}"].reshape(D, 2, INNER_E).transpose(1, 0, 2)
        both = np.concatenate([t[f"L1_ffn_w_{name}"], shared])
        return both.reshape(ES, KT, P, INNER_E).transpose(2, 0, 1, 3).reshape(P, ES, D)

    down = np.concatenate([t["L1_ffn_w_down"], t["L1_ffn_ws_down"].reshape(2, INNER_E, D)]).transpose(1, 0, 2)
    expert = np.concatenate([experts("gate"), experts("up"), down], axis=2)
    w3 = t["L3_ffn_qweights"].transpose(0, 2, 1).reshape(6, KT, P, D).transpose(2, 0, 1, 3).reshape(P, -1)
    scale3 = t["L3_ffn_scales"].transpose(2, 0, 1).reshape(KT, P // GROUP, 6 * D)
    ctx = t["ctx_1024"]
    ctx_t = heads_inside(ctx, 2).reshape(STEPS, TOK, KT, P).transpose(0, 3, 2, 1).reshape(STEPS, P, -1)
    mask = t["mask_BxSxS2_ik0"]
    out = {
        "x": steps(t["x"]).reshape(STEPS, P, NT, D), "ctx_t": ctx_t, "ctx": steps(ctx).reshape(STEPS, P, NT, D),
        "mask": steps(mask), "mask_t": steps(mask.transpose(0, 2, 1)),
        "w": w, "wo": wo, "vec": vec, "col": col, "gate": rows(t["L1_ffn_gate_w"].T),
        "expert": expert,
        "wq_gate": rows(t["L2_ffn_w_gate"].T), "wq_up": rows(t["L2_ffn_w_up"].T), "wq_down": rows(t["L2_ffn_w_down"].T),
        "w3": w3, "scale3": scale3, "la": t["L3_ffn_lora_a"].transpose(1, 0, 2).reshape(R_LORA, -1),
        "lb": t["L3_ffn_lora_b"].transpose(2, 0, 1).reshape(R_LORA, -1),
    }
    return {n: np.ascontiguousarray(a) for n, a in out.items()}


def kernel(**inputs):
    import numpy as np
    import concourse.bacc as bacc
    from concourse.bass_utils import run_bass_kernel_spmd

    arrays = lay_out(inputs)
    known = None
    for _ in range(2):
        nc = bacc.Bacc("TRN2", target_bir_lowering=False, num_devices=1)
        args = [nc.dram_tensor(f"in_{n}", a.shape, mybir.dt.from_np(a.dtype), kind="ExternalInput").ap()
                for n, a in arrays.items()]
        out = nc.dram_tensor("out", (STEPS, P, NT, D), F32, kind="ExternalOutput").ap()
        known = build(nc, known, *args, out)
    r = run_bass_kernel_spmd(nc, [{f"in_{n}": a for n, a in arrays.items()}], core_ids=[0])
    out = np.asarray(r.results[0]["out"]).reshape(STEPS, P, NB, SJ, D)
    return np.ascontiguousarray(out.transpose(0, 2, 3, 1, 4)).reshape(B, S, D)
```

```python
from contextlib import ExitStack

import concourse.bass as bass
from concourse import mybir

F32 = mybir.dt.float32
BF16 = mybir.dt.bfloat16
I32 = mybir.dt.int32
ALU = mybir.AluOpType
ACT = mybir.ActivationFunctionType
AX = mybir.AxisListType

P = 128
B, S, D = 8, 256, 256
KT = D // P
H, DH = 16, 16
NB = 2
STEPS = B // NB
TOK = NB * S
NT = TOK // P
SJ = S // P
E, TOP_K, INNER_E = 16, 2, 128
ES = E + 2
AHEAD = 4
RING = 6
INNER = 1024
R_LORA = 32
GROUP = 16
NBLK = 3
HG = 4
HPG = H // HG
DPAD = 32
SPLIT_Q = (0, 0, 1, 0, 1, 2)
SPLIT_K = (0, 1, 0, 2, 1, 0)
NSPLIT = len(SPLIT_Q)
KROWS = NSPLIT * DH
KALL = KROWS + 2
NEG = -1e30
SCALE = DH ** -0.5
ROUND = 1.5 * 2.0 ** 23
LN_EPS = 1e-5
L2_EPS = 1e-6
CLIP = 1e-5
Q_MAX = 127.0

W_L0Q, W_L0K, W_L0V, W_L0F, W_L1Q, W_L1K, W_L1V, W_L2Q, W_L2K, W_L2V = range(10)
W_QKV = ((W_L0Q, W_L0K, W_L0V), (W_L1Q, W_L1K, W_L1V), (W_L2Q, W_L2K, W_L2V))
(V_L0BV, V_L0BO, V_L1BV, V_L1BO, V_L2BQ, V_L2BK, V_L2BV, V_L2VS, V_L2VB, V_L2BO, V_L3B) = range(11)
V_BV = (V_L0BV, V_L1BV)
V_BO = (V_L0BO, V_L1BO, V_L2BO)
N_VEC = V_L3B + 6
C_L1BQ, C_L1BK, C_QS, C_QB, C_KS, C_KB, C_G, C_BETA = 0, 1, 2, 3, 4, 5, 6, 9
N_COL = 12


class Signal:

    def __init__(self, sem, known, unit=1, head=0):
        self.sem, self.known, self.unit, self.head, self.order = sem, known, unit, head, {}

    def step(self, key):
        self.order.setdefault(key, len(self.order))
        return self.sem, self.unit

    def at(self, i, key):
        if self.known is None:
            return self.sem, 1
        done = self.unit * (self.known[key] + 1) + self.head
        return self.sem, done if i is None else i * (self.unit * len(self.known)) + done

    def before(self, i):
        assert self.head
        return self.sem, i * (self.unit * len(self.known or [0])) + self.head


def build(nc, known, x_d, ctx_t_d, ctx_d, mask_d, mask_t_d, w_d, wo_d, vec_d, col_d, gate_d,
          expert_d, wq_gate_d, wq_up_d, wq_down_d, w3_d, scale3_d, la_d, lb_d, out_d):
    made = {}
    with ExitStack() as ctx:
        def sb(name, shape, dt=F32):
            return ctx.enter_context(nc.sbuf_tensor(name, shape, dt))

        def signal(name, unit=1, head=0):
            made[name] = Signal(ctx.enter_context(nc.semaphore(name)),
                                None if known is None else known[name], unit, head)
            return made[name]

        w = sb("w", [P, 10, KT, D])
        wo = sb("wo", [P, 3, KT, D])
        vec = sb("vec", [P, N_VEC, D])
        col = sb("col", [P, N_COL, KT])
        gate_w = sb("gate_w", [P, KT, E])
        expert = sb("expert", [P, RING, 3 * D])
        wq_gate = sb("wq_gate", [P, KT, INNER], BF16)
        wq_up = sb("wq_up", [P, KT, INNER], BF16)
        wq_down = sb("wq_down", [P, INNER // P, D], BF16)
        w3 = sb("w3", [P, 2 * NBLK, KT, D])

        ident = sb("ident", [P, P])
        ident_b = sb("ident_b", [P, P], BF16)
        ones = sb("ones", [P, P])
        diag_s = sb("diag_s", [P, 3, P], BF16)
        diag_t = sb("diag_t", [P, 3, P], BF16)
        neg_half = sb("neg_half", [P, NT])

        x = sb("x", [P, NT, D])
        ctx_t = sb("ctx_t", [P, NB, KT, S])
        ctx_n = sb("ctx_n", [P, NT, D])
        mask_s = sb("mask_s", [P, NB, SJ, S], BF16)
        mask_t = sb("mask_t", [P, NB, SJ, S], BF16)
        xn = sb("xn", [P, NT, D])
        xn_t = sb("xn_t", [P, NB, KT, S])
        q_st = sb("q_st", [P, NB, H // 2, 2, S], BF16)
        k_st = sb("k_st", [P, NB, H // 2, 2, S], BF16)
        qf = sb("qf", [P, NB, 2, S])
        parts = sb("parts", [P, 3, NB, 2, S], BF16)
        v = sb("v", [P, NT, H, DPAD])
        probs = sb("probs", [P, 2 * HPG, SJ * S])
        o_raw = sb("o_raw", [P, 2, S])
        work = sb("work", [P, NB, 2, SJ * D])
        hid_q = sb("hid_q", [P, NT, INNER], BF16)
        neg_max = sb("neg_max", [P, HG, HPG * SJ])
        max_row = sb("max_row", [HPG * SJ, HG, 2, P], BF16)
        sum_inv = sb("sum_inv", [P, 2, SJ, HPG])

        bn = sb("bn", [P, NT, 6])
        mv = sb("mv", [P, NT, 2])
        var_eps = sb("var_eps", [P, NT])
        rstd = sb("rstd", [P, NT])
        neg_mean = sb("neg_mean", [P, NT])
        shift = sb("shift", [P, NT])
        logit = sb("logit", [P, NT, E])
        lneg = sb("lneg", [P, NT])
        lsum = sb("lsum", [P, NT])
        score = sb("score", [P, NT, E + 8])
        top = sb("top", [P, NT, 8])
        wanted = sb("wanted", [P, NT, 8])
        marked = sb("marked", [P, NT, E + 8])
        combine = sb("combine", [P, NT, E])
        amax = sb("amax", [P, NT])
        qscale = sb("qscale", [P, NT])
        dq_gate = sb("dq_gate", [P, NT])
        dq_up = sb("dq_up", [P, NT])
        hmax = sb("hmax", [P, NT])
        hscale = sb("hscale", [P, NT])
        dq_down = sb("dq_down", [P, NT])
        held = sb("held", [P, 1])
        wsum = sb("wsum", [P, 3])
        w_unit = sb("w_unit", [P, 3])
        w_scale = sb("w_scale", [P, 3])

        mask_int = [hid_q[:, 2 * n:2 * n + 2, :].bitcast(I32).rearrange("p a t -> p (a t)") for n in range(2)]
        silu_g = [probs[:, n // 2, (n % 2) * S:(n % 2 + 1) * S] for n in range(AHEAD * NB)]
        act_e = [probs[:, HPG + n // 2, (n % 2) * S:(n % 2 + 1) * S] for n in range(AHEAD * NB)]
        hid = expert[:, :, :].rearrange("p r c -> p (r c)")
        hid = [hid[:, T * INNER:(T + 1) * INNER] for T in range(NT)]
        hid_t = [work[:, T // SJ, T % SJ, :].bitcast(BF16).rearrange("p (k t) -> p k t", k=INNER // P) for T in range(NT)]
        y_tok, v_tok = [[work[:, s, n, :].rearrange("p (a d) -> p a d", a=SJ) for s in range(NB)] for n in range(2)]
        o_tok = y_tok
        y_t = o_t = [work[:, s, 1, :].rearrange("p (k t) -> p k t", k=KT) for s in range(NB)]
        h_tok = ctx_n
        xq = [parts[:, 0, s, :, :] for s in range(NB)]
        xq_t = [parts[:, 1, s, :, :] for s in range(NB)]
        raw_w = [probs[:, 0:4, :].rearrange("p a t -> p (a t)"), probs[:, 4:8, :].rearrange("p a t -> p (a t)"),
                 work[:, :, :, :].rearrange("p a b t -> p (a b t)")]
        scale3 = k_st[:, :, :, :, :].bitcast(F32).rearrange("p s h m t -> p (s h m t)")[:, 0:KT * 6 * D].rearrange(
            "p (k n o) -> p k n o", k=KT, n=6)
        lora = q_st[:, :, :, :, :].bitcast(F32).rearrange("p s h m t -> p (s h m t)")
        la = lora[0:R_LORA, 0:6 * D].rearrange("r (n d) -> r n d", n=6)
        lb = lora[0:R_LORA, 6 * D:12 * D].rearrange("r (n d) -> r n d", n=6)

        def mine(s):
            return slice(s * SJ, (s + 1) * SJ)

        ps = ctx.enter_context(nc.psum_tensor("ps", [P, 8, 512], F32))
        filled = [signal(f"filled{b}") for b in range(8)]
        drained = [signal(f"drained{b}", head=1) for b in range(8)]
        bank_of, last_in = {}, {}
        banks = {"s": (0, 1), "m": (2, 3), "o": (4,), "c": (5, 6, 7), "up": (0, 1, 2, 3), "down": (4, 5, 6, 7),
                 "opening": (0, 1, 2, 3), "rest": (5, 6), "output": (7,)}
        own_use = {("k", 0, 0): "opening", ("v", 0, 0): "opening", ("xt", "l0a", 0): "opening", ("q", 0, 0): "opening",
                   ("k", 0, 1): "rest", ("v", 0, 1): "rest", ("xt", "l0a", 1): "rest", ("q", 0, 1): "rest",
                   ("xt", "l3f", 1): "rest"}
        own_use.update({("ot", 0, 0, hg): "output" for hg in range(HG)})
        own_use.update({(name, n, s): "rest" for name in ("h", "y", "yt", "z") for n in range(NBLK) for s in range(NB)})
        before = {}
        turn = {use: 0 for use in banks}

        def claim(pe, i, key, use="c"):
            if key not in bank_of:
                use = own_use.get(key, use)
                bank = bank_of[key] = banks[use][turn[use] % len(banks[use])]
                turn[use] += 1
                before[key] = last_in.get(bank)
                last_in[bank] = key
            bank = bank_of[key]
            if before[key] is None:
                pe.wait_ge(*drained[bank].before(i))
            else:
                pe.wait_ge(*drained[bank].at(i, before[key]))
            drained[bank].step(key)
            return ps[:, bank, :]

        def tile_of(key):
            return ps[:, bank_of[key], :]

        def tile_filled(key):
            return filled[bank_of[key]].step(key)

        def tile_drained(key):
            return drained[bank_of[key]].sem, 1

        def wait_filled(eng, i, key):
            eng.wait_ge(*filled[bank_of[key]].at(i, key))

        def wait_drained(eng, i, key):
            eng.wait_ge(*drained[bank_of[key]].at(i, key))

        def wait_all_drained(eng, i, keys):
            for key in {bank_of[key]: key for key in keys}.values():
                wait_drained(eng, i, key)

        load = {n: signal("load_" + n, 16) for n in (
            "w", "wo", "vec", "col", "gate", "wq_gate", "wq_up", "wq_down",
            "w3", "scale3", "la", "lb")}
        const_ready = signal("const_ready")
        abs_sum = signal("abs_sum")
        sum_all = signal("sum_all")
        prep = signal("prep")
        lora_done = signal("lora_done")
        lora_used = signal("lora_used")

        def per_stream(name, unit=1, head=0):
            return [signal(f"{name}{s}", unit, head) for s in range(NB)]

        x_in = per_stream("x_in", 16)
        ctx_in = per_stream("ctx_in", 16)
        ctxn_in = per_stream("ctxn_in", 16)
        mask_in = signal("mask_in", 16)
        expert_in = [signal(f"expert_in{r}", 16) for r in range(RING)]
        mask_ready = signal("mask_ready")
        x_bias = per_stream("x_bias")
        ln_stats = per_stream("ln_stats")
        ln_moments = per_stream("ln_moments")
        ln_var = per_stream("ln_var")
        ln_rstd = per_stream("ln_rstd")
        ln_shift = per_stream("ln_shift")
        ln_done = per_stream("ln_done")
        tok_made = signal("tok_made")
        part_hi = per_stream("part_hi")
        part_rest = per_stream("part_rest")
        part_mid = per_stream("part_mid")
        part_lo = per_stream("part_lo")
        stacked = {what: per_stream(f"stacked_{what}", 16) for what in "qk"}
        v_ready = per_stream("v_ready")
        max_hi = signal("max_hi")
        max_in = [signal(f"max_in{n}", 16) for n in range(2)]
        pv_done = signal("pv_done")
        inverted = signal("inverted")
        o_ready = signal("o_ready")
        route = signal("route")
        route_exp = signal("route_exp")
        silu_done = signal("silu_done")
        quant = signal("quant")
        xq_ready = signal("xq_ready")
        hid_ready = signal("hid_ready")
        stored = per_stream("stored", 16, head=16)

        block = ctx.enter_context(nc.Block())

        A, B = range(NB)

        def attention(part, L, s):
            part.maxima(L, s, 0)
            yield 0
            part.rows(L, s, 0)
            yield 1
            part.maxima(L, s, 1)
            yield 2
            part.rows(L, s, 1)
            yield 3
            part.mixed(L, s, 0)
            yield 4
            part.rows(L, s, 2)
            yield 5
            part.mixed(L, s, 1)
            yield 6
            part.rows(L, s, 3)
            yield 7
            part.values(L, s, 0)
            yield 8
            part.scores(L, s, 2)
            yield 9
            part.values(L, s, 1)
            yield 10
            part.output(L, s, 0)
            yield 11
            part.scores(L, s, 3)
            yield 12
            part.values(L, s, 2)
            yield 13
            part.output(L, s, 1)
            yield 14
            part.values(L, s, 3)
            yield 15
            part.output(L, s, 2)
            yield 16
            part.output(L, s, 3)
            yield 17

        def beside_next(part, gap, s):
            if gap == 0:
                part.project_in(0, s)
            elif gap == 2:
                part.project_out(0, s)
                part.project_add(0, s)
                part.ln("l0f", s)
            elif gap == 4:
                part.apply("l0f", s)
                part.kv(1, s)
                part.turn("l0f", s)
            elif gap == 6:
                part.ffn0(s)
            elif gap == 7:
                part.ffn0_add(s)
                part.ln("l1a", s)
            elif gap == 9:
                part.apply("l1a", s)
            elif gap == 11:
                part.turn("l1a", s)
                part.q(1, s)

        def beside_quantised(part, gap, s):
            if gap == 0:
                part.project_in(2, s)
            elif gap == 2:
                part.project_out(2, s)
                part.project_add(2, s)
                part.ln("l2f", s)
            elif gap == 4:
                part.apply("l2f", s)
                part.kv(3, s)
            elif gap == 5:
                part.quantise(s)
            elif gap == 6:
                part.quantised(s)
            elif gap == 7:
                part.hidden(s * SJ)
            elif gap == 8:
                part.hidden(s * SJ + 1)
            elif gap == 10:
                part.down(s * SJ)
            elif gap == 11:
                part.down(s * SJ + 1)
                part.ln("l3a", s)
            elif gap == 13:
                part.apply("l3a", s)
            elif gap == 14:
                part.turn("l3a", s)
                part.q(3, s)

        def opening(part):
            part.load(A)
            yield 0
            part.ln("l0a", A)
            yield 1
            part.kv(0, A)
            yield 2
            part.apply("l0a", A)
            yield 3
            part.turn("l0a", A)
            yield 4
            part.q(0, A)
            yield 5
            for gap in attention(part, 0, A):
                if gap == 7:
                    part.load(B)
                elif gap == 11:
                    part.kv(0, B)
                elif gap == 12:
                    part.ln("l0a", B)
                elif gap == 14:
                    part.apply("l0a", B)
                    part.turn("l0a", B)
                elif gap == 16:
                    part.q(0, B)
                yield 6 + gap

        def layers(part):
            part.others()
            for gap in attention(part, 0, B):
                beside_next(part, gap, A)
            for gap in attention(part, 1, A):
                beside_next(part, gap, B)
            for e in range(RING):
                part.expert(e)
            for gap in attention(part, 1, B):
                if gap == 0:
                    part.project_in(1, A)
                elif gap == 2:
                    part.project_out(1, A)
                    part.project_add(1, A)
                    part.ln("l1f", A)
                elif gap == 4:
                    part.apply("l1f", A)
                elif gap == 6:
                    part.turn("l1f", A)
                elif gap == 9:
                    part.logits(A)
                    part.masks()
                elif gap == 11:
                    part.route(A)
            part.moe()
            for gap in attention(part, 2, A):
                if gap == 0:
                    part.apply("q", B)
                elif gap == 2:
                    part.q_turn(B)
            for gap in attention(part, 2, B):
                beside_quantised(part, gap, A)
            for gap in attention(part, 3, A):
                beside_quantised(part, gap, B)
            for gap in attention(part, 3, B):
                if gap == 0:
                    part.ln("l3f", A)
                elif gap == 2:
                    part.apply("l3f", A)
                    part.turn("l3f", A)
                elif gap == 4:
                    part.block_in(0, A)
                elif gap == 6:
                    part.apply(("y", 0), A)
                    part.block_turn(0, A)
                elif gap == 9:
                    part.block_out(0, A)
                elif gap == 11:
                    part.block_in(1, A)
                elif gap == 12:
                    part.apply(("y", 1), A)
                    part.block_turn(1, A)
                elif gap == 14:
                    part.block_out(1, A)
                elif gap == 16:
                    part.block_in(2, A)

        def closing(part):
            yield 0
            rest(part, -1)
            yield 1
            for gap in opening(part):
                yield 0
                rest(part, gap)
                yield 1

        def rest(part, gap):
            if gap == -1:
                part.ln("l3f", B)
                part.apply(("y", 2), A)
                part.block_turn(2, A)
                part.apply("l3f", B)
                part.turn("l3f", B)
                part.block_out(2, A)
                part.store(A)
                part.block_in(0, B)
            elif gap == 0:
                part.apply(("y", 0), B)
                part.block_turn(0, B)
                part.block_out(0, B)
            elif gap == 2:
                part.block_in(1, B)
            elif gap == 5:
                part.apply(("y", 1), B)
                part.block_turn(1, B)
                part.block_out(1, B)
            elif gap == 6:
                part.block_in(2, B)
            elif gap == 8:
                part.apply(("y", 2), B)
                part.block_turn(2, B)
            elif gap == 10:
                part.block_out(2, B)
                part.store(B)

        def moe_order(part):
            lead = 4
            items = [(e, A) for e in range(lead)]
            for e in range(ES):
                items += [(e, B)] + ([(e + lead, A)] if e + lead < ES else [])
            beside_experts(part, -2)
            part.up(*items[0])
            beside_experts(part, -1)
            part.up(*items[1])
            for n, item in enumerate(items):
                beside_experts(part, 2 * n)
                if n + 2 < len(items):
                    part.up(*items[n + 2])
                beside_experts(part, 2 * n + 1)
                part.expert_down(*item)
            beside_experts(part, 2 * len(items))

        def beside_experts(part, gap):
            if gap == -1:
                part.project_in(1, B)
            elif gap == 0:
                part.project_out(1, B)
                part.project_add(1, B)
                part.ln("l1f", B)
            elif gap == 2:
                part.apply("l1f", B)
            elif gap == 4:
                part.turn("l1f", B)
            elif gap == 6:
                part.logits(B)
                part.route(B)
            elif gap == 14:
                part.kv(2, A)
            elif gap == 16:
                part.apply("k", A)
            elif gap == 18:
                part.kv_turn(A)
            elif gap == 22:
                part.kv_value(A)
            elif gap == 24:
                part.apply("v", A)
            elif gap == 26:
                part.value_scale(A)
            elif gap == 30:
                part.kv(2, B)
            elif gap == 32:
                part.apply("k", B)
            elif gap == 34:
                part.kv_turn(B)
            elif gap == 38:
                part.kv_value(B)
            elif gap == 40:
                part.apply("v", B)
            elif gap == 42:
                part.value_scale(B)
            elif gap == 64:
                part.ln("l2a", A)
            elif gap == 66:
                part.apply("l2a", A)
                part.turn("l2a", A)
                part.q(2, A)
            elif gap == 68:
                part.apply("q", A)
            elif gap == 70:
                part.q_turn(A)
            elif gap == 72:
                part.ln("l2a", B)
                part.apply("l2a", B)
                part.turn("l2a", B)
                part.q(2, B)

        CAUSAL = (True, True, False, False)

        def diag_kind(L, j):
            return 2 if L == 1 else (1 if j == 0 else 0)

        def split_source(what, L, s):
            if L == 2:
                return (what + "t", L, s)
            if L == 3:
                return ("xt", "l3a", s) if what == "q" else None
            return (what, L, s)

        def split_bias(what, m):
            c = C_L1BQ if what == "q" else C_L1BK
            return col[:, c, m:m + 1]

        def item_no(e, s):
            return e % AHEAD * NB + s

        @block.tensor
        def _(pe):
            mm = nc.tensor.matmul

            pe.wait_ge(*const_ready.at(None, "last"))
            pe.wait_ge(*abs_sum.at(None, 2))
            mm(ps[:, 0, 0:3], ones[:, :], wsum[:, :], start=True, stop=True).then_inc(*sum_all.step("all"))
            pe.wait_ge(*load["la"].at(None, 0))
            pe.wait_ge(*load["lb"].at(None, 0))
            for n in range(2 * NBLK):
                bank = 1 + n
                for kt in range(KT):
                    last = mm(ps[:, bank, kt * D:(kt + 1) * D], la[:, n, kt * P:(kt + 1) * P], lb[:, n, :],
                              start=True, stop=True)
                last.then_inc(*lora_done.step(n))
            pe.wait_ge(*load["w"].at(None, 0))
            pe.wait_ge(*prep.at(None, "last"))
            pe.wait_ge(*const_ready.at(None, "k_ones"))

            i = 0

            def feature_out(key, wn, act_t):
                t = claim(pe, i, key)
                for m in range(2):
                    for kt in range(KT):
                        last = mm(t[:, m * S:(m + 1) * S], w[:, wn, kt, m * P:(m + 1) * P], act_t[:, kt, :],
                                  start=kt == 0, stop=kt == KT - 1)
                last.then_inc(*tile_filled(key))

            def token_out(key, weight, act_t):
                t = claim(pe, i, key)
                for a in range(SJ):
                    for kt in range(KT):
                        last = mm(t[:, a * D:(a + 1) * D], act_t[:, kt, a * P:(a + 1) * P], weight[:, kt, :],
                                  start=kt == 0, stop=kt == KT - 1)
                last.then_inc(*tile_filled(key))

            def turn_tokens(key, tok):
                t = claim(pe, i, key)
                for kt in range(KT):
                    for a in range(SJ):
                        last = nc.tensor.transpose(t[:, kt * S + a * P:kt * S + (a + 1) * P],
                                                   tok[:, a, kt * P:(kt + 1) * P], ident[:, :])
                last.then_inc(*tile_filled(key))

            def head(t, s, h, rows, c0, n):
                return t[0:rows, s, h // 2, h % 2, c0:c0 + n]

            def score_for_max(L, s, hg, h4):
                causal = CAUSAL[L]
                h = hg * HPG + h4
                key = ("m", L, s, hg, h4)
                t = claim(pe, i, key, "m")
                for j in (range(SJ) if not causal else (1, 0)):
                    n = S if j or not causal else P
                    c0 = j * S if not causal else (0 if j else S)
                    last = mm(t[:, c0:c0 + n], head(q_st, s, h, KROWS, j * P, P), head(k_st, s, h, KROWS, 0, n),
                              start=True, stop=L == 3)
                    if causal:
                        last = mm(t[:, c0 + n - P:c0 + n], ident_b[:, :], diag_s[:, diag_kind(L, j), :],
                                  start=False, stop=True)
                    elif L == 2:
                        last = mm(t[:, c0:c0 + n], ident_b[:, :], mask_s[:, s, j, :], start=False, stop=True)
                last.then_inc(*tile_filled(key))

            def turn_max(L, s, hg):
                wait_drained(pe, i, ("m", L, s, hg, HPG - 1))
                t = claim(pe, i, ("t", L, s, hg), "m")
                nc.tensor.transpose(t[0:HPG * SJ, 0:P], neg_max[:, hg, :], ident[:, :]).then_inc(
                    *tile_filled(("t", L, s, hg)))

            def score(L, s, hg, h4):
                causal = CAUSAL[L]
                if h4 == 0:
                    pe.wait_ge(*max_in[hg % 2].at(i, (L, s, hg, 1)))
                h = hg * HPG + h4
                key = ("s", L, s, hg, h4)
                t = claim(pe, i, key, "s")
                for j in range(SJ):
                    skip = P if j and causal else 0
                    n = S - skip
                    last = mm(t[:, j * S:j * S + n], head(k_st, s, h, KALL, j * P, P), head(q_st, s, h, KALL, skip, n),
                              start=True, stop=L == 3)
                    if causal:
                        last = mm(t[:, j * S:j * S + P], ident_b[:, :], diag_t[:, diag_kind(L, j), :],
                                  start=False, stop=True)
                    elif L == 2:
                        last = mm(t[:, j * S:j * S + n], ident_b[:, :], mask_t[:, s, j, :], start=False, stop=True)
                last.then_inc(*tile_filled(key))

            def values_of(L, s, hg):
                if hg == 0:
                    if L < 2:
                        wait_drained(pe, i, ("v", L, s))
                    else:
                        pe.wait_ge(*v_ready[s].at(i, (L, s, SJ - 1)))
                t = claim(pe, i, ("o", L, s, hg), "o")
                wait_all_drained(pe, i, [("s", L, s, hg, h4) for h4 in range(HPG)])
                for j in range(SJ):
                    skip = P if j and CAUSAL[L] else 0
                    for h4 in range(HPG):
                        last = mm(t[h4 * DPAD:(h4 + 1) * DPAD, skip:S], v[:, s * SJ + j, hg * HPG + h4, :],
                                  probs[:, (hg % 2) * HPG + h4, j * S:(j + 1) * S - skip],
                                  start=j == 0, stop=j == SJ - 1, tile_position=(0, h4 * DPAD),
                                  skip_group_check=True)
                last.then_inc(*pv_done.step((L, s, hg)))

            def turn_output(L, s, hg):
                wait_drained(pe, i, ("o", L, s, hg))
                t = claim(pe, i, ("ot", L, s, hg))
                for a in range(SJ):
                    last = nc.tensor.transpose(t[:, a * P:(a + 1) * P], o_raw[:, hg % 2, a * P:(a + 1) * P], ident[:, :])
                last.then_inc(*tile_filled(("ot", L, s, hg)))

            class Part:
                def load(s):
                    pass

                apply = value_scale = masks = store = route = others = ln = quantise = expert = project_add = ffn0_add = lambda *_: None

                def kv(L, s):
                    if L == 3:
                        return
                    if L == 0:
                        pe.wait_ge(*ctx_in[s].at(i, 0))
                    if L < 2:
                        feature_out(("k", L, s), W_QKV[L][1], ctx_t[:, s, :, :])
                    else:
                        token_out(("k", L, s), w[:, W_L2K, :, :], ctx_t[:, s, :, :])
                    if L < 2:
                        token_out(("v", L, s), w[:, W_QKV[L][2], :, :], ctx_t[:, s, :, :])

                def kv_value(s):
                    token_out(("v", 2, s), w[:, W_L2V, :, :], ctx_t[:, s, :, :])

                def kv_turn(s):
                    pe.wait_ge(*ln_done[s].at(i, ("k", s, SJ - 1)))
                    turn_tokens(("kt", 2, s), y_tok[s])

                def turn(p, s):
                    pe.wait_ge(*ln_done[s].at(i, (p, s, SJ - 1)))
                    turn_tokens(("xt", p, s), (h_tok if p == "l3f" else xn)[:, mine(s), :])

                def q(L, s):
                    if L == 3:
                        return
                    wait_drained(pe, i, ("xt", f"l{L}a", s))
                    if L < 2:
                        feature_out(("q", L, s), W_QKV[L][0], xn_t[:, s, :, :])
                    else:
                        token_out(("q", L, s), w[:, W_L2Q, :, :], xn_t[:, s, :, :])

                def q_turn(s):
                    pe.wait_ge(*ln_done[s].at(i, ("q", s, SJ - 1)))
                    turn_tokens(("qt", 2, s), y_tok[s])

                def maxima(L, s, hg):
                    if hg == 0:
                        pe.wait_ge(*stacked["k"][s].at(i, (L, NSPLIT - 1)))
                        pe.wait_ge(*stacked["q"][s].at(i, (L, NSPLIT - 1)))
                        if L == 2:
                            pe.wait_ge(*mask_ready.at(i, 1))
                    for h4 in range(HPG):
                        score_for_max(L, s, hg, h4)

                def rows(L, s, hg):
                    turn_max(L, s, hg)

                def scores(L, s, hg):
                    for h4 in range(HPG):
                        score(L, s, hg, h4)

                def mixed(L, s, hg):
                    for h4 in range(HPG):
                        score(L, s, hg, h4)
                        score_for_max(L, s, hg + 2, h4)

                def values(L, s, hg):
                    values_of(L, s, hg)

                def output(L, s, hg):
                    turn_output(L, s, hg)

                def project_in(L, s):
                    if L == 3:
                        return
                    wait_drained(pe, i, ("ot", L, s, HG - 1))
                    turn_tokens(("op", L, s), o_tok[s])

                def project_out(L, s):
                    pe.wait_ge(*load["wo"].at(None, 0))
                    wait_drained(pe, i, ("op", L, s))
                    token_out(("wo", L, s), wo[:, L, :, :], o_t[s])

                def ffn0(s):
                    wait_drained(pe, i, ("xt", "l0f", s))
                    token_out(("f0", s), w[:, W_L0F, :, :], xn_t[:, s, :, :])

                def logits(s):
                    wait_drained(pe, i, ("xt", "l1f", s))
                    pe.wait_ge(*load["gate"].at(None, 0))
                    t = claim(pe, i, ("logit", s))
                    for a in range(SJ):
                        for kt in range(KT):
                            last = mm(t[:, a * E:(a + 1) * E], xn_t[:, s, kt, a * P:(a + 1) * P], gate_w[:, kt, :],
                                      start=kt == 0, stop=kt == KT - 1)
                    last.then_inc(*tile_filled(("logit", s)))

                def moe():
                    moe_order(Part)

                def up(e, s):
                    wait_drained(pe, i, ("xt", "l1f", s))
                    pe.wait_ge(*expert_in[e % RING].at(i, e))
                    t = claim(pe, i, ("eu", e, s), "up")
                    for n in range(2):
                        for kt in range(KT):
                            c0 = n * D + kt * INNER_E
                            last = mm(t[:, n * S:(n + 1) * S], expert[:, e % RING, c0:c0 + INNER_E], xn_t[:, s, kt, :],
                                      start=kt == 0, stop=kt == KT - 1)
                    last.then_inc(*tile_filled(("eu", e, s)))

                def expert_down(e, s):
                    wait_drained(pe, i, ("eu", e, s))
                    t = claim(pe, i, ("ed", e, s), "down")
                    for a in range(SJ):
                        last = mm(t[:, a * D:(a + 1) * D], act_e[item_no(e, s)][:, a * P:(a + 1) * P],
                                  expert[:, e % RING, 2 * D:3 * D], start=True, stop=True)
                    last.then_inc(*tile_filled(("ed", e, s)))

                def quantised(s):
                    pe.wait_ge(*xq_ready.at(i, (s, SJ - 1)))
                    t = claim(pe, i, ("xq", s)).bitcast(BF16)
                    for kt in range(KT):
                        for a in range(SJ):
                            last = nc.tensor.transpose(t[:, kt * S + a * P:kt * S + (a + 1) * P],
                                                       xq[s][:, a, kt * P:(kt + 1) * P], ident_b[:, :])
                    last.then_inc(*tile_filled(("xq", s)))

                def hidden(T):
                    s, a = divmod(T, SJ)
                    wait_drained(pe, i, ("xq", s))
                    for c in range(2):
                        for name, weight in (("hg", wq_gate), ("hu", wq_up)):
                            t = claim(pe, i, (name, T, c))
                            for kt in range(KT):
                                last = mm(t, xq_t[s][:, kt, a * P:(a + 1) * P], weight[:, kt, c * 512:(c + 1) * 512],
                                          start=kt == 0, stop=kt == KT - 1)
                            last.then_inc(*tile_filled((name, T, c)))

                def down(T):
                    pe.wait_ge(*hid_ready.at(i, T))
                    t = claim(pe, i, ("ht", T)).bitcast(BF16)
                    for k in range(INNER // P):
                        last = nc.tensor.transpose(t[:, k * P:(k + 1) * P], hid_q[:, T, k * P:(k + 1) * P], ident_b[:, :])
                    last.then_inc(*tile_filled(("ht", T)))
                    t = claim(pe, i, ("hd", T))
                    wait_drained(pe, i, ("ht", T))
                    for k in range(INNER // P):
                        last = mm(t[:, 0:D], hid_t[T][:, k, :], wq_down[:, k, :], start=k == 0, stop=k == INNER // P - 1)
                    last.then_inc(*tile_filled(("hd", T)))

                def block_in(n, s):
                    if n:
                        wait_drained(pe, i, ("z", n - 1, s))
                        turn_tokens(("h", n, s), h_tok[:, mine(s), :])
                    wait_drained(pe, i, ("h", n, s) if n else ("xt", "l3f", s))
                    token_out(("y", n, s), w3[:, 2 * n, :, :], xn_t[:, s, :, :])

                def block_turn(n, s):
                    pe.wait_ge(*ln_done[s].at(i, (("y", n), s, SJ - 1)))
                    turn_tokens(("yt", n, s), xn[:, mine(s), :])

                def block_out(n, s):
                    wait_drained(pe, i, ("yt", n, s))
                    token_out(("z", n, s), w3[:, 2 * n + 1, :, :], y_t[s])

            for _ in opening(Part):
                continue
            with pe.Fori(0, STEPS) as step:
                i = step
                layers(Part)
                for ahead in closing(Part):
                    i = step + 1 if ahead else step

        @block.scalar
        def _(act):
            act.wait_ge(*prep.at(None, "last"))
            act.wait_ge(*load["col"].at(None, 0))
            i = 0

            def drain(key, out):
                wait_filled(act, i, key)
                nc.scalar.activation(out, tile_of(key).rearrange("p (k t) -> p k t", t=S), ACT.Copy).then_inc(*tile_drained(key))

            def split_hi(what, L, s):
                if what == "q":
                    act.wait_ge(*part_lo[s].at(i, ("k", L, s)))
                    act.wait_ge(*stacked["k"][s].at(i, (L, NSPLIT - 1)))
                key = split_source(what, L, s)
                hi = parts[:, 0, s, :, :]
                if key is None:
                    nc.scalar.activation(hi, ctx_t[:, s, :, :], ACT.Copy).then_inc(*part_hi[s].step((what, L, s)))
                    return
                wait_filled(act, i, key)
                t = tile_of(key).rearrange("p (k t) -> p k t", t=S)
                if L == 1:
                    for m in range(2):
                        done = nc.scalar.activation(hi[:, m, :], t[:, m, :], ACT.Identity, bias=split_bias(what, m))
                    done.then_inc(*part_hi[s].step((what, L, s)))
                elif L == 2:
                    scale, bias = (C_KS, C_KB) if what == "k" else (C_QS, C_QB)
                    for m in range(2):
                        done = nc.scalar.activation(qf[:, s, m, :], t[:, m, :], ACT.Identity, scale=col[:, scale, m:m + 1],
                                                    bias=col[:, bias, m:m + 1])
                    done.then_inc(*tile_drained(key))
                    wait_drained(act, i, key)
                    nc.scalar.activation(hi, qf[:, s, :, :], ACT.Copy).then_inc(*part_hi[s].step((what, L, s)))
                else:
                    nc.scalar.activation(hi, t, ACT.Copy).then_inc(*part_hi[s].step((what, L, s)))

            def normalise(key, s, src, dst, heads_last=False):
                act.wait_ge(*ln_shift[s].at(i, (key, s)))
                for a in range(SJ):
                    T = s * SJ + a
                    out, inp = dst[:, a, :], src[:, a, :]
                    if heads_last:
                        out = out.rearrange("p (m d h) -> p h m d", m=2, d=DH)
                        inp = inp.rearrange("p (h m d) -> p h m d", m=2, d=DH)
                    nc.scalar.activation(out, inp, ACT.Identity, scale=rstd[:, T:T + 1], bias=shift[:, T:T + 1]).then_inc(
                        *ln_done[s].step((key, s, a)))

            def exps(L, s, hg):
                width = SJ * S - P if CAUSAL[L] else SJ * S
                for h4 in range(HPG):
                    key = ("s", L, s, hg, h4)
                    wait_filled(act, i, key)
                    nc.scalar.activation(probs[:, (hg % 2) * HPG + h4, 0:width], tile_of(key)[:, 0:width],
                                         ACT.Exp, scale=SCALE).then_inc(*tile_drained(key))

            class Part:
                def load(s):
                    pass

                def kv(L, s):
                    if L == 2:
                        return
                    if L == 0:
                        act.wait_ge(*ctx_in[s].at(i, 0))
                    split_hi("k", L, s)

                def kv_turn(s):
                    split_hi("k", 2, s)

                def turn(p, s):
                    if p != "l3a":
                        drain(("xt", p, s), xn_t[:, s, :, :])

                def q(L, s):
                    if L != 2:
                        split_hi("q", L, s)

                def apply(p, s):
                    if p in ("k", "q"):
                        normalise(p, s, y_tok[s], y_tok[s])
                    elif p == "v":
                        normalise(p, s, v_tok[s], v_tok[s])
                    elif p[0] == "y":
                        normalise(p, s, y_tok[s], xn[:, mine(s), :])
                    else:
                        normalise(p, s, x[:, mine(s), :], (h_tok if p == "l3f" else xn)[:, mine(s), :], heads_last=p == "l3a")

                def q_turn(s):
                    split_hi("q", 2, s)

                def scores(L, s, hg):
                    exps(L, s, hg)

                mixed = scores

                def values(L, s, hg):
                    act.wait_ge(*pv_done.at(i, (L, s, hg)))
                    nc.scalar.activation(o_raw[:, hg % 2, :], tile_of(("o", L, s, hg))[:, 0:S], ACT.Copy).then_inc(
                        *tile_drained(("o", L, s, hg)))

                def project_in(L, s):
                    if L < 3:
                        drain(("op", L, s), o_t[s])

                def logits(s):
                    pass

                def route(s):
                    act.wait_ge(*route.at(i, ("shift", s)))
                    nc.scalar.activation(logit[:, mine(s), :], logit[:, mine(s), :], ACT.Exp).then_inc(*route_exp.step(s))

                def moe():
                    moe_order(Part)

                def up(e, s):
                    n = item_no(e, s)
                    if e >= AHEAD:
                        wait_drained(act, i, ("eu", e - AHEAD, s))
                    wait_filled(act, i, ("eu", e, s))
                    nc.scalar.activation(silu_g[n], tile_of(("eu", e, s))[:, 0:S], ACT.Silu).then_inc(*silu_done.step((e, s)))

                def quantised(s):
                    wait_filled(act, i, ("xq", s))
                    nc.scalar.activation(xq_t[s], tile_of(("xq", s)).bitcast(BF16)[:, 0:KT * S].rearrange(
                        "p (k t) -> p k t", t=S), ACT.Copy).then_inc(*tile_drained(("xq", s)))

                def hidden(T):
                    act.wait_ge(*quant.at(i, ("dq_gate", T // SJ)))
                    for c in range(2):
                        wait_filled(act, i, ("hg", T, c))
                        nc.scalar.activation(hid[T][:, c * 512:(c + 1) * 512], tile_of(("hg", T, c)), ACT.Silu,
                                             scale=dq_gate[:, T:T + 1]).then_inc(*tile_drained(("hg", T, c)))

                def down(T):
                    wait_filled(act, i, ("ht", T))
                    nc.scalar.activation(hid_t[T], tile_of(("ht", T)).bitcast(BF16).rearrange(
                        "p (k t) -> p k t", k=INNER // P), ACT.Copy).then_inc(*tile_drained(("ht", T)))

                def block_in(n, s):
                    if n:
                        drain(("h", n, s), xn_t[:, s, :, :])

                def block_turn(n, s):
                    wait_filled(act, i, ("yt", n, s))
                    for kt in range(KT):
                        done = nc.scalar.activation(y_t[s][:, kt, :], tile_of(("yt", n, s))[:, kt * S:(kt + 1) * S], ACT.Gelu,
                                                    scale=col[:, C_G + n, kt:kt + 1], bias=col[:, C_BETA + n, kt:kt + 1])
                    done.then_inc(*tile_drained(("yt", n, s)))

                ln = kv_value = value_scale = masks = others = quantise = expert = maxima = rows = output = project_out = lambda *_: None
                block_out = lambda *_: None
                project_add = ffn0 = ffn0_add = expert_down = store = lambda *_: None

            for _ in opening(Part):
                continue
            with act.Fori(0, STEPS) as step:
                i = step
                layers(Part)
                for ahead in closing(Part):
                    i = step + 1 if ahead else step

        @block.vector
        def _(dve):
            V = nc.vector

            for n, name in enumerate(("wq_gate", "wq_up", "wq_down")):
                dve.wait_ge(*load[name].at(None, 0))
                V.tensor_reduce(wsum[:, n:n + 1], raw_w[n], AX.X, ALU.add, apply_absolute_value=True).then_inc(*abs_sum.step(n))
            dve.wait_ge(*sum_all.at(None, "all"))
            V.tensor_scalar(w_unit[:, :], ps[:, 0, 0:3], 1.0 / (D * INNER), CLIP, ALU.mult, ALU.max).then_inc(*prep.step("unit"))
            dve.wait_ge(*prep.at(None, "unit"))
            V.reciprocal(w_scale[:, :], w_unit[:, :]).then_inc(*prep.step("scale"))
            dve.wait_ge(*prep.at(None, "scale"))
            flat = [t[:, :, :].rearrange("p a b -> p (a b)") for t in (wq_gate, wq_up, wq_down)]
            for n in range(3):
                V.tensor_scalar(raw_w[n], raw_w[n], w_scale[:, n:n + 1], ROUND, ALU.mult, ALU.add).then_inc(*prep.step(("round", n)))
            for n in range(3):
                dve.wait_ge(*prep.at(None, ("round", n)))
                V.tensor_scalar(raw_w[n], raw_w[n], ROUND, 1.0, ALU.subtract, ALU.min).then_inc(*prep.step(("min", n)))
            for n in range(3):
                dve.wait_ge(*prep.at(None, ("min", n)))
                V.tensor_scalar(flat[n], raw_w[n], -1.0, None, ALU.max).then_inc(*prep.step(("max", n)))
            dve.wait_ge(*load["w"].at(None, 0))
            sign = w[:, W_L0F, :, :].rearrange("p k n -> p (k n)")
            below = xn[:, 0:2, :].rearrange("p a d -> p (a d)")
            V.tensor_scalar(below, sign, 0.0, None, ALU.is_lt).then_inc(*prep.step("below"))
            dve.wait_ge(*prep.at(None, "below"))
            V.scalar_tensor_tensor(sign, sign, 0.0, below, ALU.is_gt, ALU.subtract).then_inc(*prep.step("sign"))
            dve.wait_ge(*load["w3"].at(None, 0))
            dve.wait_ge(*load["scale3"].at(None, KT - 1))
            for n in range(2 * NBLK):
                V.tensor_scalar(w3[:, n, :, :], w3[:, n, :, :].bitcast(I32), 1.0 / 7.5, -1.0, ALU.mult, ALU.add).then_inc(
                    *prep.step(("deq", n)))
            for n in range(2 * NBLK):
                dve.wait_ge(*prep.at(None, ("deq", n)))
                V.tensor_tensor(w3[:, n, :, :], w3[:, n, :, :], scale3[:, :, n, :], ALU.mult).then_inc(*prep.step(("mul", n)))
            for n in range(2 * NBLK):
                dve.wait_ge(*prep.at(None, ("mul", n)))
                dve.wait_ge(*lora_done.at(None, n))
                V.tensor_tensor(w3[:, n, :, :], ps[:, 1 + n, :].rearrange("p (k o) -> p k o", k=KT), w3[:, n, :, :],
                                ALU.add).then_inc(*lora_used.step(n))
            dve.wait_ge(*lora_used.at(None, 2 * NBLK - 1))
            dve.wait_ge(*const_ready.at(None, "last"))
            V.memset(wsum[:, :], 0.0).then_inc(*prep.step("last"))
            dve.wait_ge(*prep.at(None, "last"))
            for bank in drained:
                dve.sem_inc(bank.sem, bank.head)
            dve.wait_ge(*load["vec"].at(None, 0))

            i = 0

            def hold():
                V.tensor_copy(held[:, :], neg_half[:, 0:1])

            def spread(n, many):
                return vec[:, n, :].unsqueeze(1).to_broadcast([P, many, D])

            last_norm = [None] * NB

            def moments(key, s, src, eps):
                for a in range(SJ):
                    V.bn_stats(bn[:, s * SJ + a, :], src[:, a, :]).then_inc(*ln_stats[s].step((key, s, a)))
                dve.wait_ge(*ln_stats[s].at(i, (key, s, SJ - 1)))
                if key != "l0a":
                    dve.wait_ge(*ln_done[s].at(i, (last_norm[s], s, SJ - 1)))
                last_norm[s] = key
                hold()
                for a in range(SJ):
                    V.bn_aggr(mv[:, s * SJ + a, :], bn[:, s * SJ + a, :]).then_inc(*ln_moments[s].step((key, s, a)))
                dve.wait_ge(*ln_moments[s].at(i, (key, s, SJ - 1)))
                V.tensor_scalar(neg_mean[:, mine(s)], mv[:, mine(s), 0], -1.0, None, ALU.mult)
                V.tensor_scalar(var_eps[:, mine(s)], mv[:, mine(s), 1], eps, None, ALU.add).then_inc(*ln_var[s].step((key, s)))

            def with_bias(key, n_vec, dst):
                wait_filled(dve, i, key)
                V.tensor_tensor(dst, tile_of(key).rearrange("p (a d) -> p a d", a=SJ),
                                spread(n_vec, SJ), ALU.add).then_inc(*tile_drained(key))
                wait_drained(dve, i, key)

            def split_rest(what, L, s):
                dve.wait_ge(*part_hi[s].at(i, (what, L, s)))
                key = split_source(what, L, s)
                hi, rest = parts[:, 0, s, :, :], qf[:, s, :, :]
                if L == 2 or key is None:
                    V.tensor_tensor(rest, rest if L == 2 else ctx_t[:, s, :, :], hi, ALU.subtract).then_inc(
                        *part_rest[s].step((what, L, s)))
                    dve.wait_ge(*part_rest[s].at(i, (what, L, s)))
                else:
                    t = tile_of(key).rearrange("p (k t) -> p k t", t=S)
                    if L == 1:
                        for m in range(2):
                            done = V.scalar_tensor_tensor(rest[:, m, :], t[:, m, :], split_bias(what, m), hi[:, m, :], ALU.add, ALU.subtract)
                    else:
                        done = V.tensor_tensor(rest, t, hi, ALU.subtract)
                    done.then_inc(*tile_drained(key))
                    wait_drained(dve, i, key)
                V.tensor_copy(parts[:, 1, s, :, :], rest).then_inc(*part_mid[s].step((what, L, s)))
                dve.wait_ge(*part_mid[s].at(i, (what, L, s)))
                V.tensor_tensor(parts[:, 2, s, :, :], rest, parts[:, 1, s, :, :], ALU.subtract).then_inc(*part_lo[s].step((what, L, s)))

            def add(key, s, out=x, base=x):
                wait_filled(dve, i, key)
                V.tensor_tensor(out[:, mine(s), :], tile_of(key).rearrange("p (a d) -> p a d", a=SJ), base[:, mine(s), :],
                                ALU.add).then_inc(*tile_drained(key))

            def wait_x(p, s):
                if p == "l0a":
                    dve.wait_ge(*x_in[s].at(i, 0))
                elif p in ("l0f", "l1f", "l2f"):
                    wait_drained(dve, i, ("wo", int(p[1]), s))
                elif p == "l1a":
                    wait_drained(dve, i, ("f0", s))
                elif p == "l2a":
                    wait_drained(dve, i, ("ed", ES - 1, s))
                elif p == "l3a":
                    wait_all_drained(dve, i, [("hd", s * SJ + a) for a in range(SJ)])
                elif p == "l3f":
                    dve.wait_ge(*o_ready.at(i, s))

            def reduce_maxima(L, s, hg):
                for h4 in range(HPG):
                    key = ("m", L, s, hg, h4)
                    wait_filled(dve, i, key)
                    c = h4 * SJ
                    if CAUSAL[L]:
                        V.tensor_reduce(neg_max[:, hg, c + 1:c + 2], tile_of(key)[:, 0:S], AX.X, ALU.max, negate=True)
                        done = V.tensor_reduce(neg_max[:, hg, c:c + 1], tile_of(key)[:, S:S + P], AX.X, ALU.max, negate=True)
                    else:
                        done = V.tensor_reduce(neg_max[:, hg, c:c + 2], tile_of(key).rearrange("p (j t) -> p j t", j=SJ),
                                               AX.X, ALU.max, negate=True)
                    done.then_inc(*tile_drained(key))

            def max_rows(L, s, hg):
                key = ("t", L, s, hg)
                wait_filled(dve, i, key)
                t = tile_of(key)[0:HPG * SJ, 0:P]
                V.tensor_copy(max_row[:, hg, 0, :], t).then_inc(*max_hi.step((L, s, hg)))
                dve.wait_ge(*max_hi.at(i, (L, s, hg)))
                V.tensor_tensor(max_row[:, hg, 1, :], t, max_row[:, hg, 0, :], ALU.subtract).then_inc(*tile_drained(key))

            def normalise(L, s, hg):
                key = ("ot", L, s, hg)
                wait_filled(dve, i, key)
                t = tile_of(key)[:, 0:SJ * P].rearrange("p (a h e) -> p a h e", a=SJ, e=DPAD)
                inv = sum_inv[:, hg % 2, :, :]
                V.reciprocal(inv, t[:, :, :, DH]).then_inc(*inverted.step((L, s, hg)))
                dve.wait_ge(*inverted.at(i, (L, s, hg)))
                out = o_tok[s][:, :, hg * HPG * DH:(hg + 1) * HPG * DH].rearrange("p a (h d) -> p a h d", d=DH)
                V.tensor_tensor(out, t[:, :, :, 0:DH], inv.unsqueeze(3).to_broadcast([P, SJ, HPG, DH]), ALU.mult).then_inc(
                    *tile_drained(key))
                if hg == HG - 1:
                    wait_drained(dve, i, key)

            class Part:
                def load(s):
                    pass

                def masks():
                    dve.wait_ge(*mask_in.at(i, 1))
                    for n, out in enumerate((mask_s, mask_t)):
                        V.tensor_scalar(out[:, :, :, :].rearrange("p b j t -> p (b j t)"), mask_int[n], 0, NEG,
                                        ALU.is_equal, ALU.mult).then_inc(*mask_ready.step(n))

                def kv(L, s):
                    if L < 2:
                        split_rest("k", L, s)
                        wait_filled(dve, i, ("v", L, s))
                        for a in range(SJ):
                            done = V.tensor_tensor(
                                v[:, s * SJ + a, :, 0:DH],
                                tile_of(("v", L, s))[:, a * D:(a + 1) * D].rearrange("p (h d) -> p h d", d=DH),
                                vec[:, V_BV[L], :].rearrange("p (h d) -> p h d", d=DH), ALU.add)
                        done.then_inc(*tile_drained(("v", L, s)))
                    elif L == 2:
                        with_bias(("k", L, s), V_L2BK, y_tok[s])
                        moments("k", s, y_tok[s], L2_EPS)
                    else:
                        split_rest("k", L, s)
                        dve.wait_ge(*ctxn_in[s].at(i, 0))
                        dve.wait_ge(*pv_done.at(i, (L - 1, s, HG - 1)))
                        for a in range(SJ):
                            V.tensor_copy(v[:, s * SJ + a, :, 0:DH], ctx_n[:, s * SJ + a, :].rearrange(
                                "p (h d) -> p h d", d=DH)).then_inc(*v_ready[s].step((L, s, a)))

                def kv_value(s):
                    with_bias(("v", 2, s), V_L2BV, v_tok[s])
                    moments("v", s, v_tok[s], L2_EPS)

                def value_scale(s):
                    dve.wait_ge(*ln_done[s].at(i, ("v", s, SJ - 1)))
                    V.tensor_tensor(v_tok[s], v_tok[s], spread(V_L2VS, SJ), ALU.mult).then_inc(*tok_made.step(s))
                    dve.wait_ge(*tok_made.at(i, s))
                    for a in range(SJ):
                        V.tensor_tensor(v[:, s * SJ + a, :, 0:DH], v_tok[s][:, a, :].rearrange("p (h d) -> p h d", d=DH),
                                        vec[:, V_L2VB, :].rearrange("p (h d) -> p h d", d=DH), ALU.add).then_inc(
                            *v_ready[s].step((2, s, a)))

                def kv_turn(s):
                    split_rest("k", 2, s)

                def ln(p, s):
                    wait_x(p, s)
                    moments(p, s, x[:, mine(s), :], LN_EPS)

                def q(L, s):
                    if L == 2:
                        with_bias(("q", L, s), V_L2BQ, y_tok[s])
                        moments("q", s, y_tok[s], L2_EPS)
                    else:
                        split_rest("q", L, s)

                def q_turn(s):
                    split_rest("q", 2, s)

                def maxima(L, s, hg):
                    reduce_maxima(L, s, hg)

                def mixed(L, s, hg):
                    reduce_maxima(L, s, hg + 2)

                def rows(L, s, hg):
                    max_rows(L, s, hg)

                def output(L, s, hg):
                    normalise(L, s, hg)
                    if L == 3 and hg == HG - 1:
                        V.tensor_tensor(x[:, mine(s), :], x[:, mine(s), :], o_tok[s], ALU.add).then_inc(
                            *o_ready.step(s))

                def project_add(L, s):
                    dve.wait_ge(*x_bias[s].at(i, (L, s)))
                    add(("wo", L, s), s)

                def ffn0_add(s):
                    add(("f0", s), s)

                def logits(s):
                    pass

                def route(s):
                    sl = mine(s)
                    wait_filled(dve, i, ("logit", s))
                    V.tensor_copy(logit[:, sl, :], tile_of(("logit", s))[:, 0:SJ * E].rearrange("p (t e) -> p t e", e=E)).then_inc(
                        *tile_drained(("logit", s)))
                    wait_drained(dve, i, ("logit", s))
                    V.tensor_reduce(lneg[:, sl], logit[:, sl, :], AX.X, ALU.max).then_inc(*route.step(("max", s)))
                    dve.wait_ge(*route.at(i, ("max", s)))
                    V.tensor_tensor(logit[:, sl, :], logit[:, sl, :], lneg[:, sl].unsqueeze(2).to_broadcast([P, SJ, E]),
                                    ALU.subtract).then_inc(*route.step(("shift", s)))
                    dve.wait_ge(*route_exp.at(i, s))
                    V.tensor_reduce(lsum[:, sl], logit[:, sl, :], AX.X, ALU.add).then_inc(*route.step(("sum", s)))
                    dve.wait_ge(*route.at(i, ("sum", s)))
                    V.reciprocal(lsum[:, sl], lsum[:, sl]).then_inc(*route.step(("inverse", s)))
                    dve.wait_ge(*route.at(i, ("inverse", s)))
                    V.tensor_tensor(score[:, sl, 0:E], logit[:, sl, :], lsum[:, sl].unsqueeze(2).to_broadcast([P, SJ, E]),
                                    ALU.mult).then_inc(*route.step(("score", s)))
                    dve.wait_ge(*route.at(i, ("score", s)))
                    hold()
                    for a in range(SJ):
                        V.max(top[:, s * SJ + a, :], score[:, s * SJ + a, 0:E]).then_inc(*route.step(("top", s, a)))
                    dve.wait_ge(*route.at(i, ("top", s, SJ - 1)))
                    V.tensor_copy(wanted[:, sl, 0:TOP_K], top[:, sl, 0:TOP_K]).then_inc(*route.step(("wanted", s)))
                    dve.wait_ge(*route.at(i, ("wanted", s)))
                    hold()
                    for a in range(SJ):
                        T = s * SJ + a
                        V.match_replace(marked[:, T, :], wanted[:, T, :], score[:, T, :], 2.0).then_inc(*route.step(("mark", s, a)))
                    dve.wait_ge(*route.at(i, ("mark", s, SJ - 1)))
                    V.scalar_tensor_tensor(combine[:, sl, :], marked[:, sl, 0:E], 1.5, score[:, sl, 0:E], ALU.is_ge,
                                           ALU.mult).then_inc(*route.step(("combine", s)))
                    dve.wait_ge(*route.at(i, ("combine", s)))

                def moe():
                    moe_order(Part)

                def up(e, s):
                    n = item_no(e, s)
                    dve.wait_ge(*silu_done.at(i, (e, s)))
                    V.tensor_tensor(act_e[n], tile_of(("eu", e, s))[:, S:2 * S], silu_g[n], ALU.mult).then_inc(
                        *tile_drained(("eu", e, s)))

                def expert_down(e, s):
                    wait_filled(dve, i, ("ed", e, s))
                    if e == 0:
                        dve.wait_ge(*ln_done[s].at(i, ("l1f", s, SJ - 1)))
                    else:
                        wait_drained(dve, i, ("ed", e - 1, s))
                    for a in range(SJ):
                        T = s * SJ + a
                        part = tile_of(("ed", e, s))[:, a * D:(a + 1) * D]
                        if e < E:
                            done = V.scalar_tensor_tensor(x[:, T, :], part, combine[:, T, e:e + 1], x[:, T, :],
                                                          ALU.mult, ALU.add)
                        else:
                            done = V.tensor_tensor(x[:, T, :], part, x[:, T, :], ALU.add)
                    done.then_inc(*tile_drained(("ed", e, s)))

                def quantise(s):
                    sl = mine(s)
                    dve.wait_ge(*ln_done[s].at(i, ("l2f", s, SJ - 1)))
                    V.tensor_reduce(amax[:, sl], xn[:, sl, :], AX.X, ALU.max, apply_absolute_value=True).then_inc(*quant.step(("amax", s)))
                    dve.wait_ge(*quant.at(i, ("amax", s)))
                    V.tensor_scalar(amax[:, sl], amax[:, sl], CLIP, 1.0 / Q_MAX, ALU.max, ALU.mult).then_inc(*quant.step(("clip", s)))
                    dve.wait_ge(*quant.at(i, ("clip", s)))
                    V.reciprocal(qscale[:, sl], amax[:, sl]).then_inc(*quant.step(("scale", s)))
                    V.tensor_scalar(dq_up[:, sl], amax[:, sl], w_unit[:, 1:2], None, ALU.mult).then_inc(*quant.step(("dq_up", s)))
                    V.tensor_scalar(dq_gate[:, sl], amax[:, sl], w_unit[:, 0:1], None, ALU.mult).then_inc(*quant.step(("dq_gate", s)))
                    dve.wait_ge(*quant.at(i, ("dq_gate", s)))
                    for a in range(SJ):
                        T = s * SJ + a
                        V.tensor_scalar(xn[:, T, :], xn[:, T, :], qscale[:, T:T + 1], ROUND, ALU.mult, ALU.add).then_inc(
                            *quant.step(("round", T)))
                    dve.wait_ge(*stacked["k"][s].at(i, (3, NSPLIT - 1)))
                    for a in range(SJ):
                        T = s * SJ + a
                        dve.wait_ge(*quant.at(i, ("round", T)))
                        V.tensor_scalar(xq[s][:, a, :], xn[:, T, :], ROUND, Q_MAX, ALU.subtract, ALU.min).then_inc(
                            *xq_ready.step((s, a)))

                def hidden(T):
                    h = hid[T]
                    for c in range(2):
                        wait_drained(dve, i, ("hg", T, c))
                        wait_filled(dve, i, ("hu", T, c))
                        cs = h[:, c * 512:(c + 1) * 512]
                        V.scalar_tensor_tensor(cs, tile_of(("hu", T, c)), dq_up[:, T:T + 1], cs, ALU.mult, ALU.mult).then_inc(
                            *tile_drained(("hu", T, c)))
                    wait_all_drained(dve, i, [("hu", T, c) for c in range(2)])
                    hm = hmax[:, T:T + 1]
                    V.tensor_reduce(hm, h, AX.X, ALU.max, apply_absolute_value=True).then_inc(*quant.step(("hmax", T)))
                    dve.wait_ge(*quant.at(i, ("hmax", T)))
                    V.tensor_scalar(hm, hm, CLIP, 1.0 / Q_MAX, ALU.max, ALU.mult).then_inc(*quant.step(("hclip", T)))
                    dve.wait_ge(*quant.at(i, ("hclip", T)))
                    V.reciprocal(hscale[:, T:T + 1], hm).then_inc(*quant.step(("hscale", T)))
                    V.tensor_scalar(dq_down[:, T:T + 1], hm, w_unit[:, 2:3], None, ALU.mult).then_inc(*quant.step(("dqd", T)))
                    dve.wait_ge(*quant.at(i, ("dqd", T)))
                    V.tensor_scalar(h, h, hscale[:, T:T + 1], ROUND, ALU.mult, ALU.add).then_inc(*quant.step(("hround", T)))
                    dve.wait_ge(*quant.at(i, ("hround", T)))
                    V.tensor_scalar(hid_q[:, T, :], h, ROUND, Q_MAX, ALU.subtract, ALU.min).then_inc(*hid_ready.step(T))

                def down(T):
                    wait_filled(dve, i, ("hd", T))
                    V.scalar_tensor_tensor(x[:, T, :], tile_of(("hd", T))[:, 0:D], dq_down[:, T:T + 1], x[:, T, :],
                                           ALU.mult, ALU.add).then_inc(*tile_drained(("hd", T)))

                def block_in(n, s):
                    with_bias(("y", n, s), V_L3B + 2 * n, y_tok[s])
                    moments(("y", n), s, y_tok[s], LN_EPS)

                def block_out(n, s):
                    dve.wait_ge(*x_bias[s].at(i, ("f3", n, s)))
                    if n == NBLK - 1:
                        dve.wait_ge(*x_bias[s].at(i, ("out", s)))
                    add(("z", n, s), s, x if n == NBLK - 1 else h_tok, h_tok)

                apply = store = others = turn = quantised = expert = scores = values = project_in = project_out = ffn0 = block_turn = lambda *_: None

            for _ in opening(Part):
                continue
            with dve.Fori(0, STEPS) as step:
                i = step
                layers(Part)
                for ahead in closing(Part):
                    i = step + 1 if ahead else step

        @block.gpsimd
        def _(pool):
            G = nc.gpsimd

            def clear(key, out, value=0.0):
                G.memset(out, value).then_inc(*const_ready.step(key))

            def select(key, after, out, pattern, base, mult, op, fill):
                pool.wait_ge(*const_ready.at(None, after))
                G.affine_select(out=out, in_=out, compare_op=op, fill=fill, base=base, pattern=pattern,
                                channel_multiplier=mult).then_inc(*const_ready.step(key))

            for name, out, value in (("ident", ident[:, :], 0.0), ("ident_b", ident_b[:, :], 0.0), ("ds", diag_s[:, :, :], 0.0), ("dt", diag_t[:, :, :], 0.0), ("v", v[:, :, :, :], 0.0),
                                     ("ones", ones[:, :], 1.0), ("half", neg_half[:, :], -0.5),
                                     ("wanted", wanted[:, :, TOP_K:8], -1.0), ("score", score[:, :, E:E + 8], -1.0)):
                clear(name, out, value)
            select("ident1", "score", ident[:, :], [[-1, P]], 0, 1, ALU.not_equal, 1.0)
            select("ident_b1", "score", ident_b[:, :], [[-1, P]], 0, 1, ALU.not_equal, 1.0)
            for kind in range(3):
                strict = 0 if kind == 2 else -1
                select(("ds", kind), "score", diag_s[:, kind, :], [[-1, P]], strict, 1, ALU.is_ge, NEG)
                select(("dt", kind), "score", diag_t[:, kind, :], [[1, P]], strict, -1, ALU.is_ge, NEG)
            pool.wait_ge(*const_ready.at(None, ("dt", 2)))
            clear("open_s", diag_s[0:1, 1, 0:1])
            clear("open_t", diag_t[0:1, 1, 0:1])
            clear("last", v[:, :, :, DH:DH + 1], 1.0)
            pool.wait_ge(*prep.at(None, "last"))
            clear("k_ones", k_st[KROWS:KALL, :, :, :, :], 1.0)
            pool.wait_ge(*const_ready.at(None, "k_ones"))
            pool.wait_ge(*load["vec"].at(None, 0))

            i = 0

            def power(key, s):
                tiles = mine(s)
                pool.wait_ge(*ln_var[s].at(i, (key, s)))
                G.tensor_tensor(rstd[:, tiles], var_eps[:, tiles], neg_half[:, tiles], ALU.pow).then_inc(*ln_rstd[s].step((key, s)))
                pool.wait_ge(*ln_rstd[s].at(i, (key, s)))
                G.tensor_tensor(shift[:, tiles], neg_mean[:, tiles], rstd[:, tiles], ALU.mult).then_inc(*ln_shift[s].step((key, s)))

            class Part:
                def kv(L, s):
                    if L == 2:
                        power("k", s)

                def kv_value(s):
                    power("v", s)

                def ln(p, s):
                    power(p, s)
                    if p in ("l0a", "l1a", "l2a"):
                        L = int(p[1])
                        pool.wait_ge(*ln_done[s].at(i, (p, s, SJ - 1)))
                        G.tensor_tensor(x[:, mine(s), :], x[:, mine(s), :], vec[:, V_BO[L], :].unsqueeze(1).to_broadcast([P, SJ, D]),
                                        ALU.add).then_inc(*x_bias[s].step((L, s)))

                def q(L, s):
                    if L == 2:
                        power("q", s)

                def moe():
                    moe_order(Part)

                def block_in(n, s):
                    wait_drained(pool, i, ("h", n, s) if n else ("xt", "l3f", s))
                    G.tensor_tensor(h_tok[:, mine(s), :], h_tok[:, mine(s), :],
                                    vec[:, V_L3B + 2 * n + 1, :].unsqueeze(1).to_broadcast([P, SJ, D]),
                                    ALU.add).then_inc(*x_bias[s].step(("f3", n, s)))
                    power(("y", n), s)
                    if n == NBLK - 1:
                        pool.wait_ge(*x_bias[s].at(i, ("f3", n, s)))
                        G.tensor_tensor(h_tok[:, mine(s), :], h_tok[:, mine(s), :], x[:, mine(s), :], ALU.add).then_inc(
                            *x_bias[s].step(("out", s)))

                kv_turn = q_turn = apply = value_scale = load = others = expert = turn = masks = maxima = rows = scores = mixed = values = output = project_in = project_out = project_add = ffn0 = ffn0_add = logits = route = lambda *_: None
                mixed = up = expert_down = quantise = quantised = hidden = down = block_turn = block_out = store = lambda *_: None

            for _ in opening(Part):
                continue
            with pool.Fori(0, STEPS) as step:
                i = step
                layers(Part)
                for ahead in closing(Part):
                    i = step + 1 if ahead else step

        @block.sync
        def _(sp):
            sp.dma_start(la, la_d).then_inc(*load["la"].step(0))
            sp.dma_start(lb, lb_d).then_inc(*load["lb"].step(0))
            for name, out, src in (("wq_gate", raw_w[0], wq_gate_d), ("wq_up", raw_w[1], wq_up_d), ("wq_down", raw_w[2], wq_down_d),
                                   ("w", w[:, :, :, :].rearrange("p n k o -> p (n k o)"), w_d),
                                   ("w3", w3[:, :, :, :].bitcast(I32).rearrange("p n k o -> p (n k o)"), w3_d)):
                sp.dma_start(out, src).then_inc(*load[name].step(0))
            for kt in range(KT):
                sp.dma_start(scale3[:, kt, :, :].rearrange("p n o -> p (n o)"),
                             scale3_d[kt].unsqueeze(1).to_broadcast([P // GROUP, GROUP, 6 * D])).then_inc(*load["scale3"].step(kt))
            sp.dma_start(vec[:, :, :], vec_d.unsqueeze(0).to_broadcast([P, N_VEC, D])).then_inc(*load["vec"].step(0))
            sp.dma_start(col[:, :, :].rearrange("p n k -> p (n k)"), col_d).then_inc(*load["col"].step(0))
            sp.dma_start(wo[:, :, :, :].rearrange("p n k o -> p (n k o)"), wo_d).then_inc(*load["wo"].step(0))
            sp.dma_start(gate_w[:, :, :].rearrange("p a b -> p (a b)"), gate_d).then_inc(*load["gate"].step(0))
            for done in stored:
                sp.sem_inc(done.sem, done.head)

            i = 0

            def stack(what, L, s, st, split):
                n = 0
                for part, ready in enumerate((part_hi[s], part_mid[s], part_lo[s])):
                    sp.wait_ge(*ready.at(i, (what, L, s)))
                    for at in range(NSPLIT):
                        if split[at] == part:
                            sp.dma_start(st[at * DH:(at + 1) * DH, s, :, :, :].rearrange("d h m t -> d (h m t)"),
                                         parts[:, part, s, :, :].rearrange("p m t -> p (m t)")).then_inc(
                                *stacked[what][s].step((L, n)))
                            n += 1

            def load_expert(e):
                sp.dma_start(expert[:, e % RING, :], expert_d[:, e, :]).then_inc(*expert_in[e % RING].step(e))

            def load_max(L, s, hg):
                wait_drained(sp, i, ("t", L, s, hg))
                for n in range(2):
                    sp.dma_start(q_st[KROWS + n:KROWS + n + 1, s, 2 * hg:2 * hg + 2, :, :].rearrange("r h m t -> r (h m t)"),
                                 max_row[:, hg, n, :]).then_inc(*max_in[hg % 2].step((L, s, hg, n)))

            class Part:
                def load(s):
                    sp.wait_ge(*stored[s].before(i))
                    sp.dma_start(ctx_t[:, s, :, :].rearrange("p k t -> p (k t)"), ctx_t_d[i, s]).then_inc(*ctx_in[s].step(0))
                    sp.dma_start(x[:, mine(s), :], x_d[i, :, mine(s), :]).then_inc(*x_in[s].step(0))

                def others():
                    for n, src in enumerate((mask_d, mask_t_d)):
                        sp.dma_start(mask_int[n], src[i]).then_inc(*mask_in.step(n))
                    for n in range(NB):
                        sp.dma_start(ctx_n[:, mine(n), :], ctx_d[i, :, mine(n), :]).then_inc(*ctxn_in[n].step(0))

                def expert(e):
                    load_expert(e)

                def kv(L, s):
                    if L != 2:
                        stack("k", L, s, k_st, SPLIT_K)

                def kv_turn(s):
                    stack("k", 2, s, k_st, SPLIT_K)

                def q(L, s):
                    if L != 2:
                        stack("q", L, s, q_st, SPLIT_Q)

                def q_turn(s):
                    stack("q", 2, s, q_st, SPLIT_Q)

                def rows(L, s, hg):
                    load_max(L, s, hg)

                def moe():
                    moe_order(Part)

                def expert_down(e, s):
                    if s == NB - 1 and e + RING < ES:
                        wait_filled(sp, i, ("ed", e, s))
                        load_expert(e + RING)

                def store(s):
                    wait_drained(sp, i, ("z", NBLK - 1, s))
                    sp.dma_start(out_d[i, :, mine(s), :], x[:, mine(s), :]).then_inc(*stored[s].step(0))

                apply = value_scale = masks = ln = turn = maxima = scores = mixed = values = output = project_in = project_out = project_add = ffn0 = ffn0_add = logits = route = lambda *_: None
                mixed = up = quantise = quantised = hidden = down = kv_value = block_in = block_turn = block_out = lambda *_: None

            for _ in opening(Part):
                continue
            with sp.Fori(0, STEPS) as step:
                i = step
                layers(Part)
                for ahead in closing(Part):
                    i = step + 1 if ahead else step
            sp.wait_ge(*stacked["q"][B].at(STEPS, (0, NSPLIT - 1)))
            for done in stored:
                sp.wait_ge(done.sem, done.head + done.unit * STEPS)

    return {n: s.order for n, s in made.items()}


def heads_inside(a, axis):
    import numpy as np

    shape = a.shape
    a = a.reshape(*shape[:axis], H // 2, 2, DH, *shape[axis + 1:])
    return np.ascontiguousarray(np.moveaxis(a, axis, axis + 2)).reshape(shape)


def lay_out(t):
    import numpy as np

    t = {n: np.asarray(a) for n, a in t.items()}

    def rows(a):
        return a.reshape(-1, P, a.shape[1]).transpose(1, 0, 2).reshape(P, -1)

    def steps(a):
        return a.reshape(STEPS, NB, SJ, P, -1).transpose(0, 3, 1, 2, 4).reshape(STEPS, P, -1)

    def more(a):
        return np.concatenate([a, a[:1]])

    def perm(a):
        return heads_inside(a, a.ndim - 1)

    def qk(a):
        return perm(a)

    w_list = []
    for pre, turn in (("L0", True), ("L1", True), ("L2", False)):
        wq, wk, wv = (t[f"{pre}_xattn_{n}"].T if turn else t[f"{pre}_xattn_{n}"] for n in ("Wq", "Wk", "Wv"))
        w_list += [perm(wq), heads_inside(perm(wk), 0), heads_inside(wv, 0)]
        if pre == "L0":
            w_list.append(t["L0_ffn_weight"].T)
    w = np.concatenate([rows(a) for a in w_list], axis=1)
    wo = np.stack([t["L0_xattn_Wo"].T, t["L1_xattn_Wo"].T, t["L2_xattn_Wo"]])
    wo = np.concatenate([rows(a) for a in wo], axis=1)
    vec = np.stack([t["L0_xattn_bv"], t["L0_xattn_bo"], t["L1_xattn_bv"], t["L1_xattn_bo"], perm(t["L2_xattn_bq"]),
                    perm(t["L2_xattn_bk"]), t["L2_xattn_bv"], t["L2_xattn_vn_scale"], t["L2_xattn_vn_bias"],
                    t["L2_xattn_bo"], *t["L3_ffn_biases"]])
    col = np.stack([*(perm(t[n]) for n in ("L1_xattn_bq", "L1_xattn_bk", "L2_xattn_qn_scale", "L2_xattn_qn_bias",
                                           "L2_xattn_kn_scale", "L2_xattn_kn_bias")), *t["L3_ffn_ln_gamma"], *t["L3_ffn_ln_beta"]])
    col = col.reshape(N_COL, KT, P).transpose(2, 0, 1).reshape(P, -1)

    def experts(name):
        shared = t[f"L1_ffn_ws_{name}"].reshape(D, 2, INNER_E).transpose(1, 0, 2)
        both = np.concatenate([t[f"L1_ffn_w_{name}"], shared])
        return both.reshape(ES, KT, P, INNER_E).transpose(2, 0, 1, 3).reshape(P, ES, D)

    down = np.concatenate([t["L1_ffn_w_down"], t["L1_ffn_ws_down"].reshape(2, INNER_E, D)]).transpose(1, 0, 2)
    expert = np.concatenate([experts("gate"), experts("up"), down], axis=2)
    w3 = t["L3_ffn_qweights"].transpose(0, 2, 1).reshape(6, KT, P, D).transpose(2, 0, 1, 3).reshape(P, -1)
    scale3 = t["L3_ffn_scales"].transpose(2, 0, 1).reshape(KT, P // GROUP, 6 * D)
    ctx = t["ctx_1024"]
    ctx_t = heads_inside(ctx, 2).reshape(STEPS, NB, S, KT, P).transpose(0, 1, 4, 3, 2).reshape(STEPS, NB, P, -1)
    mask = t["mask_BxSxS2_ik0"]
    out = {
        "x": more(steps(t["x"]).reshape(STEPS, P, NT, D)), "ctx_t": more(ctx_t), "ctx": steps(ctx).reshape(STEPS, P, NT, D),
        "mask": steps(mask), "mask_t": steps(mask.transpose(0, 2, 1)),
        "w": w, "wo": wo, "vec": vec, "col": col, "gate": rows(t["L1_ffn_gate_w"].T),
        "expert": expert,
        "wq_gate": rows(t["L2_ffn_w_gate"].T), "wq_up": rows(t["L2_ffn_w_up"].T), "wq_down": rows(t["L2_ffn_w_down"].T),
        "w3": w3, "scale3": scale3, "la": t["L3_ffn_lora_a"].transpose(1, 0, 2).reshape(R_LORA, -1),
        "lb": t["L3_ffn_lora_b"].transpose(2, 0, 1).reshape(R_LORA, -1),
    }
    return {n: np.ascontiguousarray(a) for n, a in out.items()}


def kernel(**inputs):
    import numpy as np
    import concourse.bacc as bacc
    from concourse.bass_utils import run_bass_kernel_spmd

    arrays = lay_out(inputs)
    known = None
    for _ in range(2):
        nc = bacc.Bacc("TRN2", target_bir_lowering=False, num_devices=1)
        args = [nc.dram_tensor(f"in_{n}", a.shape, mybir.dt.from_np(a.dtype), kind="ExternalInput").ap()
                for n, a in arrays.items()]
        out = nc.dram_tensor("out", (STEPS, P, NT, D), F32, kind="ExternalOutput").ap()
        known = build(nc, known, *args, out)
    r = run_bass_kernel_spmd(nc, [{f"in_{n}": a for n, a in arrays.items()}], core_ids=[0])
    out = np.asarray(r.results[0]["out"]).reshape(STEPS, P, NB, SJ, D)
    return np.ascontiguousarray(out.transpose(0, 2, 3, 1, 4)).reshape(B, S, D)
```
